# Optimizing a Trainium2 kernel written in Bass

```python
import numpy as np
import jax
import jax.numpy as jnp

def _softmax(x, axis=-1):
    return jax.nn.softmax(x, axis=axis)

def _gelu(x):
    return jax.nn.gelu(x, approximate=True)

def _silu(x):
    return jax.nn.silu(x)

def _sigmoid(x):
    return jax.nn.sigmoid(x)

def _layernorm(x, axis=-1, eps=1e-05):
    m = jnp.mean(x, axis=axis, keepdims=True)
    v = jnp.var(x, axis=axis, keepdims=True)
    return (x - m) / jnp.sqrt(v + eps)

def _scatter_add(tgt, idx, src, axis=0):
    return tgt.at[idx].add(src)

def _segment_sum(src, seg, n):
    return jax.ops.segment_sum(src, seg, n)
kernel_name = 'mk_prb_d1_jaxref_r8_17feb4'

def setup_inputs(seed: int=0):
    np.random.seed(seed)
    _w = jnp.asarray

    def _L0_attn_setup():
        import jax, jax.numpy as jnp
        import numpy as np
        NUM_HEADS = 16

        def _l2_normalize_complex(z):
            n = jnp.sqrt(jnp.sum(jnp.abs(z) ** 2, axis=-1, keepdims=True))
            return z / n
        key = jax.random.key(seed)
        k1, k2, k3, k4 = jax.random.split(key, 4)
        B, S, D = (4, 512, 256)
        scale = 1.0 / np.sqrt(D)
        return {'x': jax.random.normal(k1, (B, S, D), dtype=jnp.float32), 'W_q': jax.random.normal(k2, (D, D), dtype=jnp.float32) * scale, 'W_kv': jax.random.normal(k3, (D, D), dtype=jnp.float32) * scale, 'W_o': jax.random.normal(k4, (D, D), dtype=jnp.float32) * scale}
    _L0_attn_in = _L0_attn_setup()

    def _L0_ffn_setup():
        import jax, jax.numpy as jnp
        import numpy as np
        D_MODEL = 256
        D_HIDDEN = 176
        NUM_SHARED = 2
        NUM_ROUTED = 32
        TOP_K = 6

        def _expert_apply(xf, w1, b1, w2, b2):
            return jnp.maximum(xf @ w1 + b1, 0.0) @ w2 + b2
        key = jax.random.key(seed)
        ks = jax.random.split(key, 11)
        d, h = (D_MODEL, D_HIDDEN)
        s1 = 1.0 / np.sqrt(d)
        s2 = 1.0 / np.sqrt(h)
        x = jax.random.normal(ks[0], (2, 256, d), dtype=jnp.float32)
        sw1 = jax.random.uniform(ks[1], (NUM_SHARED, d, h), jnp.float32, -s1, s1)
        sb1 = jax.random.uniform(ks[2], (NUM_SHARED, h), jnp.float32, -s1, s1)
        sw2 = jax.random.uniform(ks[3], (NUM_SHARED, h, d), jnp.float32, -s2, s2)
        sb2 = jax.random.uniform(ks[4], (NUM_SHARED, d), jnp.float32, -s2, s2)
        rw1 = jax.random.uniform(ks[5], (NUM_ROUTED, d, h), jnp.float32, -s1, s1)
        rb1 = jax.random.uniform(ks[6], (NUM_ROUTED, h), jnp.float32, -s1, s1)
        rw2 = jax.random.uniform(ks[7], (NUM_ROUTED, h, d), jnp.float32, -s2, s2)
        rb2 = jax.random.uniform(ks[8], (NUM_ROUTED, d), jnp.float32, -s2, s2)
        router_w = jax.random.uniform(ks[9], (d, NUM_ROUTED), jnp.float32, -s1, s1)
        router_b = jax.random.uniform(ks[10], (NUM_ROUTED,), jnp.float32, -s1, s1)
        return {'x': x, 'sw1': sw1, 'sb1': sb1, 'sw2': sw2, 'sb2': sb2, 'rw1': rw1, 'rb1': rb1, 'rw2': rw2, 'rb2': rb2, 'router_w': router_w, 'router_b': router_b}
    _L0_ffn_in = _L0_ffn_setup()
    _d = {'L0_attn_x': _L0_attn_in['x'], 'L0_attn_W_q': _L0_attn_in['W_q'], 'L0_attn_W_kv': _L0_attn_in['W_kv'], 'L0_attn_W_o': _L0_attn_in['W_o'], 'L0_ffn_sw1': _L0_ffn_in['sw1'], 'L0_ffn_sb1': _L0_ffn_in['sb1'], 'L0_ffn_sw2': _L0_ffn_in['sw2'], 'L0_ffn_sb2': _L0_ffn_in['sb2'], 'L0_ffn_rw1': _L0_ffn_in['rw1'], 'L0_ffn_rb1': _L0_ffn_in['rb1'], 'L0_ffn_rw2': _L0_ffn_in['rw2'], 'L0_ffn_rb2': _L0_ffn_in['rb2'], 'L0_ffn_router_w': _L0_ffn_in['router_w'], 'L0_ffn_router_b': _L0_ffn_in['router_b']}
    _x0 = _d['L0_attn_x']
    _d['L0_attn_x'] = jax.random.normal(jax.random.fold_in(jax.random.key(seed), 1), (4, 512, 256), dtype=_x0.dtype)
    del _x0
    return _d

def reference(L0_attn_x, L0_attn_W_q, L0_attn_W_kv, L0_attn_W_o, L0_ffn_sw1, L0_ffn_sb1, L0_ffn_sw2, L0_ffn_sb2, L0_ffn_rw1, L0_ffn_rb1, L0_ffn_rw2, L0_ffn_rb2, L0_ffn_router_w, L0_ffn_router_b):

    def _L0_attn_ref(x, W_q, W_kv, W_o):
        import jax, jax.numpy as jnp
        import numpy as np
        NUM_HEADS = 16

        def _l2_normalize_complex(z):
            n = jnp.sqrt(jnp.sum(jnp.abs(z) ** 2, axis=-1, keepdims=True))
            return z / n
        B, S, D = x.shape
        H = NUM_HEADS
        hd = D // H
        q = (x @ W_q.T).reshape(B, S, H, hd)
        kv = (x @ W_kv.T).reshape(B, S, H, hd)
        qf = jnp.fft.fft(q, axis=-1)
        kvf = jnp.fft.fft(kv, axis=-1)
        qf = _l2_normalize_complex(qf)
        kvf = _l2_normalize_complex(kvf)
        kvf = jnp.cumsum(kvf, axis=1)
        qv = qf * kvf
        values_hat = jnp.fft.ifft(qv, axis=-1).real.astype(x.dtype)
        values_hat = values_hat.reshape(B, S, D)
        return values_hat @ W_o.T

    def _L0_ffn_ref(x, sw1, sb1, sw2, sb2, rw1, rb1, rw2, rb2, router_w, router_b):
        import jax, jax.numpy as jnp
        import numpy as np
        D_MODEL = 256
        D_HIDDEN = 176
        NUM_SHARED = 2
        NUM_ROUTED = 32
        TOP_K = 6

        def _expert_apply(xf, w1, b1, w2, b2):
            return jnp.maximum(xf @ w1 + b1, 0.0) @ w2 + b2
        B, S, d = x.shape
        flat = x.reshape(-1, d)
        T = flat.shape[0]

        def sh_body(acc, p):
            w1, b1, w2, b2 = p
            return (acc + _expert_apply(flat, w1, b1, w2, b2), None)
        shared_out, _ = jax.lax.scan(sh_body, jnp.zeros_like(flat), (sw1, sb1, sw2, sb2))
        shared_out = shared_out / NUM_SHARED
        logits = flat @ router_w + router_b
        probs = jax.nn.softmax(logits, axis=-1)
        topk_p, topk_i = jax.lax.top_k(probs, TOP_K)
        topk_p = topk_p / jnp.sum(topk_p, axis=-1, keepdims=True)
        gates = jnp.zeros((T, NUM_ROUTED), dtype=flat.dtype)
        gates = gates.at[jnp.arange(T)[:, None], topk_i].add(topk_p)

        def r_body(acc, p):
            w1, b1, w2, b2, g = p
            return (acc + g[:, None] * _expert_apply(flat, w1, b1, w2, b2), None)
        routed_out, _ = jax.lax.scan(r_body, jnp.zeros_like(flat), (rw1, rb1, rw2, rb2, gates.T))
        return (shared_out + routed_out).reshape(B, S, d)
    x = L0_attn_x
    xn = _layernorm(x, axis=-1)
    x = x + _L0_attn_ref(xn, L0_attn_W_q, L0_attn_W_kv, L0_attn_W_o) + _L0_ffn_ref(xn, L0_ffn_sw1, L0_ffn_sb1, L0_ffn_sw2, L0_ffn_sb2, L0_ffn_rw1, L0_ffn_rb1, L0_ffn_rw2, L0_ffn_rb2, L0_ffn_router_w, L0_ffn_router_b)
    return x

_drawn_inputs = setup_inputs


def setup_inputs(seed=0):
    import zlib

    import numpy as np

    out = dict(_drawn_inputs(seed))
    spreads = {}
    factors = {'L0_ffn_sb1': 5.344, 'L0_ffn_rb1': 8.0, 'L0_ffn_rb2': 3.232, 'L0_ffn_router_b': 2.923}
    for name, (base, spread) in spreads.items():
        noise = np.random.default_rng([zlib.crc32(name.encode()), seed]).standard_normal(out[name].shape)
        drawn = base * np.exp(spread * noise) if base else spread * noise
        out[name] = jnp.asarray(drawn.astype(out[name].dtype))
    for name, factor in factors.items():
        out[name] = (out[name] * factor).astype(out[name].dtype)
    return out
```

```python
import numpy as np
from contextlib import ExitStack

import concourse.bass as bass
from concourse import mybir

F32, F16, I32, U32 = mybir.dt.float32, mybir.dt.float16, mybir.dt.int32, mybir.dt.uint32

P = 128
B, S, D = 4, 512, 256
TOK = B * S
NT = TOK // P
TB = S // P
KD = D // P
HEADS = 16
HD = D // HEADS
NF = HD // 2
E = 32
NS = 2
EA = E + NS
HID = 176
HC = HID // 2
TOPK = 6
NBLK = P
EPS = 1e-5
SC = 16.0
LNCH = 3
GS = 2
NW = EA // GS
RING = 4
assert NBLK == TOK * TOPK // P + E and NBLK % RING == 0

C_IOTA_E = 0
C_EDGE = C_IOTA_E + E
C_PIDX = C_EDGE + NT
C_TOKID = C_PIDX + 1
C_IDENT = C_TOKID + NT
C_HEADSUM = C_IDENT + P
C_ALL = C_HEADSUM + P
H_SLOT = 0
H_TRI = P
H_ONES = 2 * P
H_IDENT = 3 * P
H_ALL = 4 * P


def build(nc, a, out):
    ACT = mybir.ActivationFunctionType
    ALU = mybir.AluOpType
    AX = mybir.AxisListType.X

    ctx = ExitStack()
    with ctx:
        def sb(name, shape, dt):
            return ctx.enter_context(nc.sbuf_tensor(name, shape, dt))

        def sem(name):
            return ctx.enter_context(nc.semaphore(name))

        def cut(t, at, words, dt=F32, rows=P):
            v = t[0:rows, at:at + words]
            return v if dt == F32 else v.bitcast(dt)

        XR = sb("XR", [P, NT * D], F32)
        xn = XR[:, :].rearrange("p (t d) -> p t d", t=NT)
        xT_hi = cut(XR, 0, NT * D // 2, F16).rearrange("p (k t) -> p k t", k=KD)
        xT_lo = cut(XR, NT * D // 2, NT * D // 2, F16).rearrange("p (k t) -> p k t", k=KD)
        SR = sb("SR", [P, NT * D], F32)
        xs = cut(SR, 0, NT * D, F16).rearrange("p (t h d) -> p t h d", t=NT, h=2)
        prod32 = cut(SR, 0, LNCH * S).rearrange("p (c t) -> p c t", c=LNCH)
        h32s = cut(SR, LNCH * S, 2 * NS * S, rows=HC).rearrange("p (c t) -> p c t", c=2 * NS)
        TR = sb("TR", [P, KD * TOK], F32)
        w_raw = [cut(TR, i * KD * D, KD * D).rearrange("p (k n) -> p k n", k=KD) for i in range(3)]
        f_mat = cut(TR, 3 * KD * D, KD * D).rearrange("p (k n) -> p k n", k=KD)
        g_mat = cut(TR, 4 * KD * D, KD * LNCH * P).rearrange("p (k n) -> p k n", k=KD)
        xT32 = TR[:, :].rearrange("p (k t) -> p k t", k=KD)
        xg = cut(TR, 0, RING * D, F16).rearrange("p (r c) -> p r c", r=RING)
        xgT = cut(TR, RING * D, 2 * D, F16).rearrange("p (r c s) -> p r c s", r=2, c=4)
        h32 = cut(TR, RING * D + 2 * D, 2 * 2 * P, rows=HC).rearrange("p (r m s) -> p r m s", r=2, m=2)
        h_hi = cut(TR, RING * D + 4 * D, 2 * P, F16, rows=HC).rearrange("p (r m s) -> p r m s", r=2, m=2)
        h_lo = cut(TR, RING * D + 5 * D, 2 * P, F16, rows=HC).rearrange("p (r m s) -> p r m s", r=2, m=2)
        yb = cut(TR, RING * D + 6 * D, RING * D).rearrange("p (r n) -> p r n", r=RING)
        work = [cut(TR, i * S, S) for i in range(8)]
        W1N, W2N = EA * KD * HID, EA * 2 * D
        W1H = sb("W1H", [P, W1N // 2], F32)
        W1L = sb("W1L", [P, W1N // 2], F32)
        W2H = sb("W2H", [P, W2N // 2], F32)
        W2L = sb("W2L", [P, W2N // 2], F32)
        w1h, w1l = cut(W1H, 0, W1N // 2, F16), cut(W1L, 0, W1N // 2, F16)
        w2h, w2l = cut(W2H, 0, W2N // 2, F16, rows=HC), cut(W2L, 0, W2N // 2, F16, rows=HC)
        acc = cut(W1H, 0, NT * D).rearrange("p (t d) -> p t d", t=NT)
        q32 = cut(W1H, NT * D, 2 * S).rearrange("p (c t) -> p c t", c=2)
        rows = cut(W1L, 0, 2 * TOPK * D).rearrange("p (r k d) -> p r k d", r=2, k=TOPK)
        k32 = cut(W1L, 2 * TOPK * D, 2 * S).rearrange("p (c t) -> p c t", c=2)
        kc32 = cut(W1L, 2 * TOPK * D + 2 * S, 2 * S).rearrange("p (c t) -> p c t", c=2)
        hs_hi = cut(W2H, 0, NS * TOK, F16, rows=HC).rearrange("p (c t) -> p c t", c=2 * NS)
        hs_lo = cut(W2H, NS * TOK, NS * TOK, F16, rows=HC).rearrange("p (c t) -> p c t", c=2 * NS)
        p_hi = cut(W2L, 0, LNCH * TOK // 2, F16).rearrange("p (c t) -> p c t", c=LNCH)
        p_lo = cut(W2L, LNCH * TOK // 2, LNCH * TOK // 2, F16).rearrange("p (c t) -> p c t", c=LNCH)
        assert NT * D + 2 * S <= E * KD * HID // 2 and 2 * TOPK * D + 4 * S <= E * KD * HID // 2
        assert 2 * NS * TOK <= E * D and LNCH * TOK <= E * D
        G1, G2 = GS * KD * HID, GS * 2 * D
        GR = sb("GR", [P, 2 * (G1 + G2)], F32)
        st1 = [cut(GR, r * (G1 + G2), G1) for r in range(2)]
        st2 = [cut(GR, r * (G1 + G2) + G1, G2, rows=HC) for r in range(2)]
        gT = [cut(GR, i * TOK // 2, TOK // 2, F16, rows=E + NS) for i in range(2)]
        b2p = [sb(f"b2{h}", [E + NS, D], F16) for h in "hl"]
        aw = [[sb(f"aw{n}{h}", [P, KD, D], F16) for h in "hl"] for n in "qk"]
        bw = [sb(f"bw{h}", [P, LNCH, D], F16) for h in "hl"]
        cf = sb("cf", [P, C_ALL], F32)
        ch = sb("ch", [P, H_ALL], F16)
        rw = sb("rw", [P, KD, E], F32)
        rb = sb("rb", [P, E], F32)
        b1 = sb("b1", [HC, EA * 2], F32)
        b1s = sb("b1s", [HC, EA * 2], F32)
        b2 = sb("b2", [E + NS, D], F32)
        stats = sb("stats", [P, NT, 6], F32)
        mv = sb("mv", [P, NT, 2], F32)
        std, rstd, t16a, t16b = (sb(n, [P, NT], F32) for n in ("std", "rstd", "t16a", "t16b"))
        TE = NT * E
        OH = cut(SR, 0, TOPK * TE // 2, F16).rearrange("p (k t e) -> p k t e", k=TOPK, t=NT)
        at = TOPK * TE // 2
        dlog, prb, pos, tmp = (cut(SR, at + i * TE, TE).rearrange("p (t e) -> p t e", t=NT) for i in range(4))
        at += 4 * TE
        mask = cut(SR, at, TE // 2, F16).rearrange("p (t e) -> p t e", t=NT)
        gates = sb("gates", [P, NT, E], F32)
        m8 = sb("m8", [P, NT, 8], F32)
        i8 = sb("i8", [P, NT, 8], U32)
        i8f = sb("i8f", [P, NT, 8], F32)
        gate = sb("gate", [P, NT, TOPK], F32)
        cnt, nblk, cum, first = (sb(n, [P, E], F32) for n in ("cnt", "nblk", "cum", "first"))
        ones_e = sb("ones_e", [P, E], F32)
        posk = sb("posk", [P, TOPK, NT], F32)
        row_of = sb("row_of", [P, TOPK, NT], I32)
        slot_i = sb("slot_i", [P, 2, TOPK, NT], I32)
        slot_f = sb("slot_f", [P, 2, TOPK, NT], F32)
        NOH = 4
        oh_slot = sb("oh_slot", [P, NOH, P], F16)
        oh_blk = sb("oh_blk", [P, NOH, P], F16)
        token_of = sb("token_of", [P, NBLK], I32)
        ebc = sb("ebc", [P, 1], F32)
        expert_of = sb("expert_of", [1, NBLK], I32)
        xg_idx = sb("xg_idx", [P, RING], I32)
        row_idx = sb("row_idx", [P, 2, TOPK], I32)
        zero1 = sb("zero1", [P, 1], F32)

        xs_dram = nc.dram_tensor("xs_dram", [TOK, 2 * D], F16, kind="Internal").ap()
        y_dram = nc.dram_tensor("y_dram", [NBLK * P, D], F32, kind="Internal").ap()

        ps = [ctx.enter_context(nc.psum_tensor(f"ps{i}", [P, 512], F32)) for i in range(8)]
        ps_x = [ps[i][:, 0:D].bitcast(F16) for i in (0, 1)]
        ps_h = [ps[i][0:HC, 0:2 * P] for i in (2, 3)]
        ps_y = [ps[i][:, 0:D] for i in (4, 5)]

        ident32, headsum = cf[:, C_IDENT:C_IDENT + P], cf[:, C_HEADSUM:C_HEADSUM + P]
        slot_iota, tri, ones16, ident16 = (ch[:, i:i + P] for i in (H_SLOT, H_TRI, H_ONES, H_IDENT))

        s_x = [sem(f"s_x{g}") for g in range(B)]
        s_raw, s_const = sem("s_raw"), sem("s_const")
        s_w = [sem(f"s_w{r}") for r in range(2)]
        s_wh, s_wl = sem("s_wh"), sem("s_wl")
        s_xs, s_xsd = sem("s_xs"), sem("s_xsd")
        s_d = sem("s_d")
        s_std, s_ln = sem("s_std"), sem("s_ln")
        s_ab, s_abs = sem("s_ab"), sem("s_abs")
        s_abl = sem("s_abl")
        s_tr, s_xt = sem("s_tr"), sem("s_xt")
        s_xth, s_xtl = sem("s_xth"), sem("s_xtl")
        s_log, s_dl, s_exp = sem("s_log"), sem("s_dl"), sem("s_exp")
        s_mask, s_cnt = sem("s_mask"), sem("s_cnt")
        s_oh, s_tab = sem("s_oh"), sem("s_tab")
        s_eb, s_ebr, s_lists = sem("s_eb"), sem("s_ebr"), sem("s_lists")
        s_bias = sem("s_bias")
        s_hold = sem("s_hold")
        s_gi = sem("s_gi")
        s_g = [sem(f"s_g{r}") for r in range(RING)]
        s_T, s_X, s_H, s_R, s_C, s_S, s_L, s_Y = (sem("s_" + n) for n in "TXHRCSLY")
        s_yd = [sem(f"s_yd{r}") for r in range(RING)]
        s_acc = sem("s_acc")
        s_ri = sem("s_ri")
        s_r = [sem(f"s_r{r}") for r in range(2)]
        s_sum = sem("s_sum")
        s_gt, s_gtc, s_gtl = sem("s_gt"), sem("s_gtc"), sem("s_gtl")
        s_sp, s_spc = sem("s_sp"), sem("s_spc")
        s_sq, s_sqa, s_nm, s_rt, s_nr = sem("s_sq"), sem("s_sqa"), sem("s_nm"), sem("s_rt"), sem("s_nr")
        s_p32, s_ph, s_pl = sem("s_p32"), sem("s_ph"), sem("s_pl")
        s_sh, s_shr, s_shh, s_shl = sem("s_sh"), sem("s_shr"), sem("s_shh"), sem("s_shl")
        s_v = sem("s_v")
        s_o, s_fin = sem("s_o"), sem("s_fin")
        s_out = sem("s_out")

        N_RAW, N_CONST = 5, 8

        def hold(eng, s, value):
            eng.wait_ge(s, value)
            eng.sem_inc(s_hold, 1)

        def halves(w, at, n):
            return w[:, bass.ds(at, n)]

        with nc.Block() as block:

            @block.sync
            def _(eng):
                for dst, name in zip((*w_raw, f_mat, g_mat), ("wq", "wkv", "woT", "f_mat", "g_mat")):
                    eng.dma_start(dst, a[name]).then_inc(s_raw, 16)
                for g in range(B):
                    eng.dma_start(xn[:, g * TB:(g + 1) * TB, :],
                                  a["x"][g].rearrange("(t p) d -> p t d", p=P)).then_inc(s_x[g], 16)
                for dst, src in ((cf[:, :], a["cf"]), (ch[:, :], a["ch"]), (rw[:, :, :], a["rw"]),
                                 (rb[:, :], a["rb"].partition_broadcast(P)), (b1[:, :], a["b1"]),
                                 (b2[0:E, :], a["rb2"]), (b2[E:E + NS, :], a["sb2"])):
                    eng.dma_start(dst, src).then_inc(s_const, 16)
                eng.dma_start(zero1[:, :], a["zero"]).then_inc(s_const, 16)

                def weights(step, r):
                    eng.dma_start(st1[r], a["w1"][:, bass.ds(step * G1, G1)]).then_inc(s_w[r], 16)
                    eng.dma_start(st2[r], a["w2"][:, bass.ds(step * G2, G2)]).then_inc(s_w[r], 16)

                weights(0, 0)
                weights(1, 1)
                eng.wait_ge(s_xs, NT)
                eng.dma_start(xs_dram.rearrange("(t p) c -> p t c", p=P),
                              xs.rearrange("p t h d -> p t (h d)")).then_inc(s_xsd, 16)
                with eng.Fori(1, NW // 2) as i:
                    for r in range(2):
                        hold(eng, s_wl, 2 * i + r - 1)
                        weights(2 * i + r, r)
                for step in range(NW // 2 * 2, NW):
                    eng.wait_ge(s_wl, step - 1)
                    weights(step, step % 2)
                with eng.Fori(0, NBLK // RING) as i:
                    for r in range(RING):
                        hold(eng, s_Y, RING * i + r + 1)
                        eng.dma_start(y_dram[bass.ds((RING * i + r) * P, P), :], yb[:, r, :]).then_inc(s_yd[r], 16)
                eng.wait_ge(s_L, NBLK)
                eng.dma_start(acc, a["x"].rearrange("b (t p) d -> p (b t) d", p=P)).then_inc(s_acc, 16)
                with eng.Fori(0, NT) as t:
                    hold(eng, s_fin, t + 3)
                    eng.dma_start(out.rearrange("b s d -> (b s) d")[bass.ds(t * P, P), :],
                                  acc[:, bass.ds(t, 1), :].rearrange("p a d -> p (a d)")).then_inc(s_out, 16)
                eng.wait_ge(s_out, 16 * NT)

            @block.gpsimd
            def _(eng):
                for c in range(KD * B):
                    k, g = c // B, c % B
                    eng.wait_ge(s_xth, c + 1)
                    eng.tensor_tensor(xT_lo[:, k, g * S:(g + 1) * S], xT32[:, k, g * S:(g + 1) * S],
                                      xT_hi[:, k, g * S:(g + 1) * S], ALU.subtract).then_inc(s_xtl, 1)
                eng.wait_ge(s_lists, 2)
                eng.wait_ge(s_xsd, 16)
                eng.wait_ge(s_xtl, KD * B)
                with eng.Fori(0, NBLK // RING) as i:
                    for r in range(RING):
                        hold(eng, s_T, RING * i + r + 1)
                        eng.tensor_copy(xg_idx[:, r:r + 1], token_of[:, bass.ds(RING * i + r, 1)]).then_inc(s_gi, 1)
                        hold(eng, s_gi, RING * i + r + 1)
                        eng.indirect_dma_start(
                            out=xg[:, r, :], out_offset=None, in_=xs_dram,
                            in_offset=bass.IndirectOffsetOnAxis(ap=xg_idx[:, r:r + 1], axis=0)).then_inc(s_g[r], 16)
                for r in range(RING):
                    eng.wait_ge(s_yd[r], 16 * (NBLK // RING))
                eng.wait_ge(s_L, NBLK)
                with eng.Fori(0, NT // 2) as i:
                    for r in range(2):
                        hold(eng, s_sum, 2 * i + r + 1)
                        eng.tensor_copy(row_idx[:, r, :].unsqueeze(2), row_of[:, :, bass.ds(2 * i + r, 1)]).then_inc(s_ri, 1)
                        hold(eng, s_ri, 2 * i + r + 1)
                        for k in range(TOPK):
                            eng.indirect_dma_start(
                                out=rows[:, r, k, :], out_offset=None, in_=y_dram,
                                in_offset=bass.IndirectOffsetOnAxis(ap=row_idx[:, r, k:k + 1], axis=0)).then_inc(s_r[r], 16)

            @block.scalar
            def _(eng):
                eng.wait_ge(s_const, 16 * N_CONST)
                eng.activation(b1s[:, 0:2 * E], b1[:, 0:2 * E], ACT.Copy, scale=SC).then_inc(s_bias, 1)
                eng.activation(b1s[:, 2 * E:], b1[:, 2 * E:], ACT.Copy, scale=SC / NS).then_inc(s_bias, 1)
                for c in range(2 * KD + LNCH):
                    w, k = (aw[c // KD], c % KD) if c < 2 * KD else (bw, c - 2 * KD)
                    eng.wait_ge(s_ab, c + 1)
                    eng.activation(w[0][:, k, :], ps[c][:, 0:D], ACT.Copy, scale=SC).then_inc(s_abs, 1)
                eng.wait_ge(s_d, 1)
                eng.activation(std[:, :], t16a[:, :], ACT.Sqrt).then_inc(s_std, 1)
                eng.wait_ge(s_abl, 2 * KD + LNCH)
                for c in range(KD * B):
                    k, g = c // B, c % B
                    eng.wait_ge(s_tr, c + 1)
                    eng.activation(xT32[:, k, g * S:(g + 1) * S], ps[c % 4][:, :], ACT.Copy).then_inc(s_xt, 1)
                eng.wait_ge(s_dl, 1)
                eng.wait_ge(s_xt, KD * B)
                eng.activation(prb, dlog, ACT.Exp).then_inc(s_exp, 1)
                for c in range(KD * B):
                    k, g = c // B, c % B
                    eng.activation(xT_hi[:, k, g * S:(g + 1) * S], xT32[:, k, g * S:(g + 1) * S], ACT.Copy).then_inc(s_xth, 1)

                def high(step, r, n):
                    hold(eng, s_w[r], 32 * (n + 1))
                    eng.activation(w1h[:, bass.ds(step * G1, G1)], st1[r], ACT.Copy, scale=SC).then_inc(s_wh, 1)
                    eng.activation(w2h[:, bass.ds(step * G2, G2)], st2[r], ACT.Copy, scale=SC).then_inc(s_wh, 1)

                with eng.Fori(0, NW // 2) as i:
                    for r in range(2):
                        high(2 * i + r, r, i)
                for step in range(NW // 2 * 2, NW):
                    high(step, step % 2, step // 2)

                eng.wait_ge(s_bias, 2)
                eng.wait_ge(s_lists, 2)
                eng.wait_ge(s_xtl, KD * B)

                def relu(blk, r):
                    e = eng.value_load(expert_of[0:1, bass.ds(blk, 1)], min_val=0, max_val=E - 1)
                    hold(eng, s_H, blk + 1)
                    hold(eng, s_S, blk + 1)
                    for m in range(2):
                        eng.activation(h32[:, r % 2, m, :], ps_h[r % 2][:, m * P:(m + 1) * P], ACT.Relu,
                                       bias=b1s[:, bass.ds(2 * e + m, 1)], scale=1.0 / SC).then_inc(s_R, 1)

                def rows_out(blk, r, n):
                    hold(eng, s_L, blk + 1)
                    hold(eng, s_yd[r], 16 * n)
                    eng.activation(yb[:, r, :], ps_y[r % 2], ACT.Copy, scale=1.0 / (SC * SC)).then_inc(s_Y, 1)

                def group(i, lo):
                    for r in range(lo, RING + lo):
                        relu(RING * i + r, r)
                        rows_out(RING * i + r - 1, (r - 1) % RING, i + (r - 1) // RING)

                relu(0, 0)
                for r in range(1, RING + 1):
                    relu(r, r)
                    eng.wait_ge(s_L, r)
                    eng.activation(yb[:, r - 1, :], ps_y[(r - 1) % 2], ACT.Copy, scale=1.0 / (SC * SC)).then_inc(s_Y, 1)
                with eng.Fori(1, NBLK // RING - 1) as i:
                    group(i, 1)
                last = NBLK // RING - 1
                for r in range(1, RING):
                    relu(RING * last + r, r)
                    rows_out(RING * last + r - 1, r - 1, last)
                rows_out(NBLK - 1, RING - 1, last)

                eng.wait_ge(s_L, NBLK)
                eng.wait_ge(s_S, NBLK + 2)
                for r in range(RING):
                    eng.wait_ge(s_yd[r], 16 * (NBLK // RING))
                eng.activation(b2p[0][:, :], b2[:, :], ACT.Copy, scale=SC).then_inc(s_gtc, 1)
                for g in range(B):
                    eng.wait_ge(s_gt, g + 1)
                    eng.activation(gT[0][0:E, g * S:(g + 1) * S], ps[g][0:E, :], ACT.Copy, scale=SC).then_inc(s_gtc, 1)
                with eng.Fori(0, B) as b:
                    hold(eng, s_pl, LNCH * b + 1)
                    for c in range(4):
                        dst = (q32, k32)[c // 2][:, c % 2, :]
                        hold(eng, s_sp, 4 * b + c + 1)
                        eng.activation(dst, ps[c][:, :], ACT.Copy, scale=1.0 / (SC * SC)).then_inc(s_spc, 1)
                    for c in range(4):
                        src = (q32, k32)[c // 2][:, c % 2, :]
                        hold(eng, s_spc, 4 * b + c + 1)
                        eng.activation(work[c], src, ACT.Square).then_inc(s_sq, 1)
                    hold(eng, s_shl, 2 * NS * b + 1)
                    for c in range(2 * NS):
                        hold(eng, s_sh, 2 * NS * b + c + 1)
                        eng.activation(h32s[:, c, :], ps[6 + c % 2][0:HC, :], ACT.Relu,
                                       bias=b1s[:, 2 * E + c:2 * E + c + 1], scale=1.0 / (SC * NS)).then_inc(s_shr, 1)
                    for n in range(2):
                        hold(eng, s_nm, 2 * b + n + 1)
                        eng.activation(work[4 + n], ps[4 + n][:, :], ACT.Sqrt).then_inc(s_rt, 1)
                    for c in range(2 * NS):
                        hold(eng, s_shr, 2 * NS * b + c + 1)
                        eng.activation(hs_hi[:, c, bass.ds(b * S, S)], h32s[:, c, :], ACT.Copy).then_inc(s_shh, 1)
                    for c in range(LNCH):
                        hold(eng, s_p32, LNCH * b + c + 1)
                        eng.activation(p_hi[:, c, bass.ds(b * S, S)], prod32[:, c, :], ACT.Copy).then_inc(s_ph, 1)

            @block.vector
            def _(eng):
                n_d = [0]

                def own(ins):
                    ins.then_inc(s_d, 1)
                    n_d[0] += 1
                    eng.wait_ge(s_d, n_d[0])

                eng.sem_inc(s_S, 2)
                for t in range(NT):
                    eng.wait_ge(s_x[t // TB], 16)
                    last = eng.bn_stats(stats[:, t, :], xn[:, t, :])
                    last.then_inc(s_ln, 1)
                for t in range(NT):
                    eng.wait_ge(s_ln, t + 1)
                    eng.bn_aggr(mv[:, t, :], stats[:, t, :]).then_inc(s_ln, 1)
                eng.wait_ge(s_ln, 2 * NT)
                var = mv[:, :, 1]
                own(eng.tensor_scalar(t16a[:, :], var, EPS, None, ALU.add))
                eng.wait_ge(s_std, 1)
                own(eng.reciprocal(t16b[:, :], std[:, :]))
                own(eng.tensor_tensor(t16b[:, :], t16b[:, :], t16a[:, :], ALU.mult))
                own(eng.tensor_tensor(t16b[:, :], t16b[:, :], std[:, :], ALU.add))
                own(eng.reciprocal(rstd[:, :], t16b[:, :]))
                own(eng.tensor_scalar(rstd[:, :], rstd[:, :], 2.0 * SC, None, ALU.mult))
                n_ln = 2 * NT
                for t in range(NT):
                    eng.tensor_scalar(xn[:, t, :], xn[:, t, :], mv[:, t, 0:1], rstd[:, t:t + 1],
                                      ALU.subtract, ALU.mult).then_inc(s_ln, 1)
                for c in range(2 * KD + LNCH):
                    w, k = (aw[c // KD], c % KD) if c < 2 * KD else (bw, c - 2 * KD)
                    eng.wait_ge(s_abs, c + 1)
                    eng.scalar_tensor_tensor(w[1][:, k, :], ps[c][:, 0:D], SC, w[0][:, k, :],
                                             ALU.mult, ALU.subtract).then_inc(s_abl, 1)
                for g in range(B):
                    t = slice(g * TB, (g + 1) * TB)
                    eng.wait_ge(s_ln, n_ln + (g + 1) * TB)
                    own(eng.tensor_copy(xs[:, t, 0, :], xn[:, t, :]))
                    eng.tensor_tensor(xs[:, t, 1, :], xn[:, t, :], xs[:, t, 0, :], ALU.subtract).then_inc(s_xs, TB)

                eng.wait_ge(s_log, 1)
                eng.wait_ge(s_xsd, 16)
                own(eng.scalar_tensor_tensor(dlog, ps[4][:, :].rearrange("p (t e) -> p t e", t=NT), 1.0 / SC,
                                             rb[:, :].unsqueeze(1).to_broadcast([P, NT, E]), ALU.mult, ALU.add))
                own(eng.tensor_reduce(t16a[:, :], dlog, AX, ALU.max))
                eng.tensor_tensor(dlog, dlog, t16a[:, :].unsqueeze(2).to_broadcast([P, NT, E]),
                                  ALU.subtract).then_inc(s_dl, 1)
                eng.wait_ge(s_exp, 1)
                for t in range(NT):
                    own(eng.max(m8[:, t, :], prb[:, t, :]))
                    ins = eng.max_index(i8[:, t, :], m8[:, t, :], prb[:, t, :])
                    if t < NT - 1:
                        ins.then_inc(s_ln, 1)
                    else:
                        ins.then_inc(s_ln, 1)
                eng.wait_ge(s_ln, 4 * NT)
                own(eng.tensor_copy(i8f[:, :, :], i8[:, :, :]))
                for k in range(TOPK):
                    ins = eng.tensor_tensor(OH[:, k, :, :], cf[:, C_IOTA_E:C_IOTA_E + E].unsqueeze(1).to_broadcast([P, NT, E]),
                                            i8f[:, :, k:k + 1].to_broadcast([P, NT, E]), ALU.is_equal)
                    own(ins)
                with nc.allow_low_precision(reason="sums of zeros and at most one 1"):
                    eng.tensor_reduce(mask, OH.rearrange("p k t e -> p t e k"), AX, ALU.add).then_inc(s_mask, 1)
                own(eng.tensor_reduce(t16a[:, :], m8[:, :, 0:TOPK], AX, ALU.add))
                own(eng.reciprocal(t16b[:, :], t16a[:, :]))
                own(eng.tensor_tensor(gate[:, :, :], m8[:, :, 0:TOPK], t16b[:, :].unsqueeze(2).to_broadcast([P, NT, TOPK]), ALU.mult))
                eng.wait_ge(s_mask, 1)
                own(eng.tensor_tensor(gates[:, :, :], prb, mask, ALU.mult))
                own(eng.tensor_tensor(gates[:, :, :], gates[:, :, :], t16b[:, :].unsqueeze(2).to_broadcast([P, NT, E]), ALU.mult))
                own(eng.memset(ones_e[:, :], 1.0))
                eng.wait_ge(s_cnt, 1)
                totals = ps[6][:, :].rearrange("p (t e) -> p t e", t=NT)
                own(eng.memset(tmp[:, 0, :], 0.0))
                for t in range(NT):
                    dst = tmp[:, t + 1, :] if t < NT - 1 else cnt[:, :]
                    own(eng.tensor_tensor(dst, totals[:, t, :], tmp[:, t, :], ALU.add))
                own(eng.tensor_tensor(pos.rearrange("p t e -> p (t e)").rearrange("p (e t) -> p e t", e=E),
                                      cnt[:, :].unsqueeze(2).to_broadcast([P, E, NT]),
                                      cf[:, C_EDGE:C_EDGE + NT].unsqueeze(1).to_broadcast([P, E, NT]), ALU.is_gt))
                own(eng.tensor_reduce(nblk[:, :], pos.rearrange("p t e -> p (t e)").rearrange("p (e t) -> p e t", e=E), AX, ALU.add))
                own(eng.tensor_tensor_scan(cum[:, :], ones_e[:, :], nblk[:, :], 0.0, ALU.mult, ALU.add))
                own(eng.tensor_tensor(first[:, :], cum[:, :], nblk[:, :], ALU.subtract))
                own(eng.scalar_tensor_tensor(pos, first[:, :].unsqueeze(1).to_broadcast([P, NT, E]), float(P), tmp,
                                             ALU.mult, ALU.add))
                own(eng.tensor_tensor(pos, pos, ps[5][:, :].rearrange("p (t e) -> p t e", t=NT), ALU.add))
                for k in range(TOPK):
                    own(eng.tensor_tensor(dlog, OH[:, k, :, :], pos, ALU.mult))
                    own(eng.tensor_reduce(posk[:, k, :], dlog, AX, ALU.add))
                own(eng.tensor_copy(row_of[:, :, :], posk[:, :, :]))
                own(eng.tensor_scalar(slot_i[:, 0, :, :], row_of[:, :, :], P - 1, None, ALU.bitwise_and))
                own(eng.tensor_scalar(slot_i[:, 1, :, :], row_of[:, :, :], 7, None, ALU.logical_shift_right))
                own(eng.tensor_copy(slot_f[:, :, :, :], slot_i[:, :, :, :]))
                j = 0
                for k in range(TOPK):
                    for t in range(NT):
                        if j >= NOH:
                            eng.wait_ge(s_tab, j - NOH + 1)
                        eng.tensor_scalar(oh_slot[:, j % NOH, :], slot_iota, slot_f[:, 0, k, t:t + 1], None,
                                          ALU.is_equal).then_inc(s_oh, 1)
                        eng.tensor_scalar(oh_blk[:, j % NOH, :], slot_iota, slot_f[:, 1, k, t:t + 1],
                                          cf[:, C_TOKID + t:C_TOKID + t + 1], ALU.is_equal, ALU.mult).then_inc(s_oh, 1)
                        j += 1
                own(eng.tensor_scalar(nblk[:, :], cum[:, :], cf[:, C_PIDX:C_PIDX + 1], None, ALU.is_le))
                own(eng.tensor_reduce(first[:, 0:1], nblk[:, :], AX, ALU.add))
                eng.tensor_scalar(ebc[:, :], first[:, 0:1], float(E - 1), None, ALU.min).then_inc(s_eb, 1)
                eng.wait_ge(s_tab, NT * TOPK)
                eng.tensor_copy(token_of[:, :], ps[7][:, 0:NBLK]).then_inc(s_lists, 1)
                eng.wait_ge(s_ebr, 1)
                eng.tensor_copy(expert_of[:, :], ps[6][0:1, 0:NBLK]).then_inc(s_lists, 1)

                def low(step, r):
                    hold(eng, s_wh, 2 * step + 2)
                    eng.scalar_tensor_tensor(w1l[:, bass.ds(step * G1, G1)], st1[r], SC, w1h[:, bass.ds(step * G1, G1)],
                                             ALU.mult, ALU.subtract).then_inc(s_v, 1)
                    eng.scalar_tensor_tensor(w2l[:, bass.ds(step * G2, G2)], st2[r], SC, w2h[:, bass.ds(step * G2, G2)],
                                             ALU.mult, ALU.subtract).then_inc(s_v, 1)
                    hold(eng, s_v, 2 * step + 2)
                    eng.sem_inc(s_wl, 1)

                with eng.Fori(0, NW // 2) as i:
                    for r in range(2):
                        low(2 * i + r, r)
                for step in range(NW // 2 * 2, NW):
                    low(step, step % 2)

                def tokens_out(blk, r):
                    hold(eng, s_T, blk + RING + 1)
                    eng.tensor_copy(xgT[:, r % 2, :, :].rearrange("p c s -> p (c s)"), ps_x[r % 2]).then_inc(s_X, 1)

                def split(blk, r):
                    hold(eng, s_R, 2 * blk + 2)
                    eng.tensor_copy(h_hi[:, r % 2, :, :], h32[:, r % 2, :, :]).then_inc(s_C, 1)
                    hold(eng, s_C, blk + 1)
                    eng.tensor_tensor(h_lo[:, r % 2, :, :], h32[:, r % 2, :, :], h_hi[:, r % 2, :, :],
                                      ALU.subtract).then_inc(s_S, 1)

                eng.wait_ge(s_xtl, KD * B)
                tokens_out(0, 0)
                tokens_out(1, 1)
                with eng.Fori(0, NBLK // RING - 1) as i:
                    for r in range(RING):
                        blk = RING * i + r
                        hold(eng, s_H, blk + 1)
                        tokens_out(blk + 2, r)
                        split(blk, r)
                base = NBLK - RING
                for r in range(RING):
                    if r < RING - 2:
                        eng.wait_ge(s_H, base + r + 1)
                        tokens_out(base + r + 2, r)
                    split(base + r, r)

                eng.wait_ge(s_L, NBLK)
                eng.wait_ge(s_acc, 16)
                n_v = 2 * NW
                eng.memset(gT[0][E:E + NS, :], SC / NS).then_inc(s_gtl, 1)
                eng.memset(gT[1][E:E + NS, :], 0.0).then_inc(s_gtl, 1)
                eng.wait_ge(s_gtc, 1)
                eng.scalar_tensor_tensor(b2p[1][:, :], b2[:, :], SC, b2p[0][:, :], ALU.mult, ALU.subtract).then_inc(s_gtl, 1)
                for g in range(B):
                    eng.wait_ge(s_gtc, g + 2)
                    eng.scalar_tensor_tensor(gT[1][0:E, g * S:(g + 1) * S], ps[g][0:E, :], SC, gT[0][0:E, g * S:(g + 1) * S],
                                             ALU.mult, ALU.subtract).then_inc(s_gtl, 1)
                PER_ATT, PER_SUM = 20, TB * (TOPK - 1)

                def attention(b, n0):
                    n = [0]

                    def mine(ins):
                        ins.then_inc(s_v, 1)
                        n[0] += 1
                        hold(eng, s_v, n0 + n[0])

                    for i in range(2):
                        hold(eng, s_sq, 4 * b + 2 * i + 2)
                        eng.tensor_tensor(work[6 + i], work[2 * i], work[2 * i + 1], ALU.add).then_inc(s_sqa, 1)
                    for i, v32 in enumerate((q32, k32)):
                        hold(eng, s_rt, 2 * b + i + 1)
                        mine(eng.reciprocal(work[2 * i], work[4 + i]))
                        mine(eng.tensor_tensor(work[2 * i + 1], work[2 * i], ps[4 + i][:, :], ALU.mult))
                        mine(eng.tensor_tensor(work[2 * i + 1], work[2 * i + 1], work[4 + i], ALU.add))
                        mine(eng.reciprocal(work[2 * i], work[2 * i + 1]))
                        mine(eng.scalar_tensor_tensor(v32, v32, (SC, 1.0)[i], work[2 * i].unsqueeze(1).to_broadcast([P, 2, S]),
                                                      ALU.mult, ALU.mult))
                    eng.sem_inc(s_nr, 1)
                    mine(eng.memset(work[4], 1.0))
                    for c in range(2):
                        mine(eng.tensor_tensor_scan(kc32[:, c, :], work[4], k32[:, c, :], 0.0, ALU.mult, ALU.add))
                    hold(eng, s_ph, LNCH * b + 1)
                    mine(eng.tensor_tensor(prod32[:, 0:2, :], q32, kc32, ALU.mult))
                    mine(eng.tensor_tensor(work[0], q32[:, 0, :], kc32[:, 1, :], ALU.mult))
                    mine(eng.tensor_tensor(work[1], q32[:, 1, :], kc32[:, 0, :], ALU.mult))
                    eng.sem_inc(s_p32, 2)
                    mine(eng.tensor_tensor(prod32[:, 2, :], work[0], work[1], ALU.add))
                    eng.sem_inc(s_p32, 1)
                    for c in range(LNCH):
                        hold(eng, s_ph, LNCH * b + c + 2)
                        mine(eng.tensor_tensor(p_lo[:, c, bass.ds(b * S, S)], prod32[:, c, :], p_hi[:, c, bass.ds(b * S, S)], ALU.subtract))
                        eng.sem_inc(s_pl, 1)
                    for c in range(2 * NS):
                        hold(eng, s_shh, 2 * NS * b + c + 1)
                        eng.tensor_tensor(hs_lo[:, c, bass.ds(b * S, S)], h32s[:, c, :], hs_hi[:, c, bass.ds(b * S, S)],
                                          ALU.subtract).then_inc(s_shl, 1)
                    assert n[0] == PER_ATT, n[0]

                def sums(b, n0):
                    for tt in range(TB):
                        t, r = TB * b + tt, tt % 2
                        row = acc[:, bass.ds(t, 1), :].rearrange("p a d -> p (a d)")
                        hold(eng, s_r[r], 16 * TOPK * (TB // 2 * b + tt // 2 + 1))
                        for k in range(TOPK):
                            g = gate[:, bass.ds(t, 1), k:k + 1].rearrange("p a k -> p (a k)")
                            ins = eng.scalar_tensor_tensor(row, rows[:, r, k, :], g, row, ALU.mult, ALU.add)
                            if k < TOPK - 1:
                                ins.then_inc(s_v, 1)
                                hold(eng, s_v, n0 + (TOPK - 1) * tt + k + 1)
                            else:
                                ins.then_inc(s_sum, 1)
                        hold(eng, s_o, t + 1)
                        hold(eng, s_sum, t + 3)
                        eng.scalar_tensor_tensor(row, ps[4 + r][:, 0:D], 1.0 / (SC * SC), row,
                                                 ALU.mult, ALU.add).then_inc(s_fin, 1)

                PER = PER_ATT + PER_SUM
                attention(0, n_v)
                with eng.Fori(1, B) as b:
                    attention(b, n_v + PER_ATT + (b - 1) * PER)
                    sums(b - 1, n_v + 2 * PER_ATT + (b - 1) * PER)
                sums(B - 1, n_v + PER_ATT + (B - 1) * PER)

            @block.tensor
            def _(eng):
                eng.sem_inc(s_T, RING)
                eng.sem_inc(s_sum, 2)
                eng.sem_inc(s_pl, 1)
                eng.sem_inc(s_fin, 2)
                eng.sem_inc(s_ph, 1)
                eng.sem_inc(s_shl, 1)

                eng.wait_ge(s_raw, 16 * N_RAW)
                for c in range(2 * KD + LNCH):
                    for k in range(KD):
                        if c < 2 * KD:
                            m = c % KD
                            ins = eng.matmul(ps[c][:, 0:D], w_raw[c // KD][:, k, m * P:(m + 1) * P], f_mat[:, k, :],
                                             start=(k == 0), stop=(k == KD - 1))
                        else:
                            m = c - 2 * KD
                            ins = eng.matmul(ps[c][:, 0:D], g_mat[:, k, m * P:(m + 1) * P], w_raw[2][:, k, :],
                                             start=(k == 0), stop=(k == KD - 1))
                    ins.then_inc(s_ab, 1)

                eng.wait_ge(s_const, 16 * N_CONST)
                eng.wait_ge(s_abl, 2 * KD + LNCH)
                for c in range(KD * B):
                    k, g = c // B, c % B
                    eng.wait_ge(s_ln, 2 * NT + (g + 1) * TB)
                    if c >= 4:
                        eng.wait_ge(s_xt, c - 3)
                    for tt in range(TB):
                        ins = eng.transpose(ps[c % 4][:, tt * P:(tt + 1) * P], xn[:, g * TB + tt, k * P:(k + 1) * P], ident32)
                    ins.then_inc(s_tr, 1)
                eng.wait_ge(s_xt, KD * B)
                for t in range(NT):
                    for k in range(KD):
                        ins = eng.matmul(ps[4][:, t * E:(t + 1) * E], xT32[:, k, t * P:(t + 1) * P], rw[:, k, :],
                                         start=(k == 0), stop=(k == KD - 1))
                ins.then_inc(s_log, 1)
                eng.wait_ge(s_mask, 1)
                flat = mask.rearrange("p t e -> p (t e)")
                eng.matmul(ps[5][:, :], tri, flat, start=True, stop=True)
                eng.matmul(ps[6][:, :], ones16, flat, start=True, stop=True).then_inc(s_cnt, 1)
                for j in range(TOPK * NT):
                    eng.wait_ge(s_oh, 2 * j + 2)
                    eng.matmul(ps[7][:, 0:P], oh_slot[:, j % NOH, :], oh_blk[:, j % NOH, :],
                               start=(j == 0), stop=(j == TOPK * NT - 1)).then_inc(s_tab, 1)
                eng.wait_ge(s_eb, 1)
                eng.matmul(ps[6][0:1, 0:P], ebc[:, :], ident32, start=True, stop=True).then_inc(s_ebr, 1)

                def transposes(blk, r, n):
                    eng.wait_ge(s_g[r % RING], 16 * (n + 1))
                    for c in range(4):
                        ins = eng.transpose(ps_x[r % 2][:, c * P:(c + 1) * P], xg[:, r % RING, c * P:(c + 1) * P], ident16)
                    ins.then_inc(s_T, 1)

                def layer1(blk, r):
                    e = eng.value_load(expert_of[0:1, bass.ds(blk, 1)], min_val=0, max_val=E - 1)
                    eng.wait_ge(s_X, blk + 1)
                    for m in range(2):
                        j = 0
                        for k in range(KD):
                            for w, x_part in ((w1h, k), (w1h, KD + k), (w1l, k)):
                                ins = eng.matmul(ps_h[r % 2][:, m * P:(m + 1) * P],
                                                 w[:, bass.ds(e * (KD * HID) + k * HID + m * HC, HC)],
                                                 xgT[:, r % 2, x_part, :], start=(j == 0), stop=(j == 3 * KD - 1))
                                j += 1
                    ins.then_inc(s_H, 1)

                def layer2(blk, r):
                    e = eng.value_load(expert_of[0:1, bass.ds(blk, 1)], min_val=0, max_val=E - 1)
                    if not (isinstance(blk, int) and blk < 2):
                        eng.wait_ge(s_Y, blk - 1)
                    eng.wait_ge(s_S, blk + 3)
                    j = 0
                    for m in range(2):
                        for h, w in ((h_hi, w2h), (h_hi, w2l), (h_lo, w2h)):
                            ins = eng.matmul(ps_y[r % 2], h[:, r % 2, m, :], w[:, bass.ds(e * (2 * D) + m * D, D)],
                                             start=(j == 0), stop=(j == 5))
                            j += 1
                    ins.then_inc(s_L, 1)

                eng.wait_ge(s_wl, NW)
                eng.wait_ge(s_lists, 2)
                transposes(0, 0, 0)

                def step(blk, r, i, first=False, last=False):
                    if not last:
                        if not first:
                            eng.wait_ge(s_X, blk)
                        transposes(blk + 1, r + 1, i + (r + 1) // RING)
                    layer1(blk, r)
                    if not first:
                        layer2(blk - 1, r - 1)

                for r in range(RING):
                    step(r, r, 0, first=(r == 0))
                with eng.Fori(1, NBLK // RING - 1) as i:
                    for r in range(RING):
                        step(RING * i + r, r, i)
                for r in range(RING):
                    step(NBLK - RING + r, r, NBLK // RING - 1, last=(r == RING - 1))
                layer2(NBLK - 1, RING - 1)

                eng.wait_ge(s_R, 2 * NBLK)
                for g in range(B):
                    for tt in range(TB):
                        ins = eng.transpose(ps[g][0:E, tt * P:(tt + 1) * P], gates[:, g * TB + tt, :], ident32)
                    ins.then_inc(s_gt, 1)
                eng.wait_ge(s_gtl, 3 + B)
                eng.wait_ge(s_Y, NBLK)

                def stage1(b):
                    for c in range(4):
                        if not (isinstance(b, int) and b == 0):
                            eng.wait_ge(s_spc, 4 * b - 4 + c + 1)
                        j = 0
                        w, m = aw[c // 2], c % 2
                        for k in range(KD):
                            for wp, xp in ((w[0], xT_hi), (w[0], xT_lo), (w[1], xT_hi)):
                                ins = eng.matmul(ps[c][:, :], wp[:, k, m * P:(m + 1) * P], xp[:, k, bass.ds(b * S, S)],
                                                 start=(j == 0), stop=(j == 3 * KD - 1))
                                j += 1
                        ins.then_inc(s_sp, 1)
                    for c in range(2 * NS):
                        if not (isinstance(b, int) and b == 0 and c < 2):
                            eng.wait_ge(s_shr, 2 * NS * b + c - 1)
                        j = 0
                        at = (E + c // 2) * KD * HID + (c % 2) * HC
                        for k in range(KD):
                            for wp, xp in ((w1h, xT_hi), (w1h, xT_lo), (w1l, xT_hi)):
                                ins = eng.matmul(ps[6 + c % 2][0:HC, :], wp[:, at + k * HID:at + k * HID + HC],
                                                 xp[:, k, bass.ds(b * S, S)], start=(j == 0), stop=(j == 3 * KD - 1))
                                j += 1
                        ins.then_inc(s_sh, 1)
                    if not isinstance(b, int):
                        eng.wait_ge(s_fin, TB * (b - 1) + 2)
                    for n in range(2):
                        eng.wait_ge(s_sqa, 2 * b + n + 1)
                        eng.matmul(ps[4 + n][:, :], headsum, work[6 + n], start=True, stop=True).then_inc(s_nm, 1)

                def stage2(b, read):
                    eng.wait_ge(s_pl, LNCH * b + LNCH + 1)
                    eng.wait_ge(s_shl, 2 * NS * b + 2 * NS + 1)
                    eng.wait_ge(s_nr, read)
                    for tt in range(TB):
                        t = TB * b + tt
                        eng.wait_ge(s_fin, t + 1)
                        tok = bass.ds(t * P, P)
                        parts = [(p_, w[:, c, :], c) for c in range(LNCH) for p_, w in ((p_hi, bw[0]), (p_hi, bw[1]), (p_lo, bw[0]))]
                        for c in range(2 * NS):
                            at = (2 * E + c) * D
                            parts += [(h_, w[:, at:at + D], c) for h_, w in ((hs_hi, w2h), (hs_hi, w2l), (hs_lo, w2h))]
                        parts += [(g_.unsqueeze(1), b_[:, :], 0) for g_, b_ in ((gT[0], b2p[0]), (gT[0], b2p[1]), (gT[1], b2p[0]))]
                        for j, (lhs, rhs, c) in enumerate(parts):
                            ins = eng.matmul(ps[4 + tt % 2][:, 0:D], lhs[:, c, tok], rhs, start=(j == 0), stop=(j == len(parts) - 1))
                        ins.then_inc(s_o, 1)

                stage1(0)
                with eng.Fori(1, B) as b:
                    stage1(b)
                    stage2(b - 1, b + 1)
                stage2(B - 1, B)


def constants():
    cf = np.zeros((P, C_ALL), np.float32)
    p = np.arange(P)
    cf[:, C_IOTA_E:C_IOTA_E + E] = np.arange(E)
    cf[:, C_EDGE:C_EDGE + NT] = np.arange(NT) * P
    cf[:, C_PIDX] = p
    cf[:, C_TOKID:C_TOKID + NT] = np.arange(NT)[None, :] * P + p[:, None]
    cf[:, C_IDENT:C_IDENT + P] = np.eye(P)
    cf[:, C_HEADSUM:C_HEADSUM + P] = (p[:, None] // NF) == (p[None, :] // NF)
    ch = np.zeros((P, H_ALL), np.float16)
    ch[:, H_SLOT:H_SLOT + P] = p
    ch[:, H_TRI:H_TRI + P] = p[:, None] < p[None, :]
    ch[:, H_ONES:H_ONES + P] = 1
    ch[:, H_IDENT:H_IDENT + P] = np.eye(P)
    i, f = np.arange(HD)[:, None], np.arange(NF)[None, :]
    ang = 2 * np.pi * i * f / HD
    alt = (-1.0) ** np.arange(HD)
    re = np.sqrt(2.0 / HD) * np.cos(ang)
    im = -np.sqrt(2.0 / HD) * np.sin(ang)
    re[:, 0] = 1 / np.sqrt(HD)
    im[:, 0] = alt / np.sqrt(HD)
    rr, ii, ri = np.cos(ang) / HD, -np.cos(ang) / HD, -np.sin(ang) / HD
    ii[:, 0] = alt / HD
    ri[:, 0] = 0
    fm = np.zeros((HEADS, HD, 2, HEADS, NF))
    gm = np.zeros((HEADS, HD, LNCH, HEADS, NF))
    for h in range(HEADS):
        for c, m in enumerate((re, im)):
            fm[h, :, c, h, :] = m
        for c, m in enumerate((rr, ii, ri)):
            gm[h, :, c, h, :] = 4 * m
    chunk = lambda m: np.ascontiguousarray(m.reshape(KD, P, -1).transpose(1, 0, 2).astype(np.float32))
    return {"cf": cf, "ch": ch, "f_mat": chunk(fm), "g_mat": chunk(gm), "zero": np.zeros((P, 1), np.float32)}


def kernel(**inputs):
    import concourse.bacc as bacc
    from concourse.bass_utils import run_bass_kernel_spmd

    v = {n.replace("L0_", ""): np.asarray(t) for n, t in inputs.items()}
    lay = np.ascontiguousarray
    chunk = lambda m: lay(m.reshape(KD, P, -1).transpose(1, 0, 2))
    w1 = np.concatenate([v["ffn_rw1"], v["ffn_sw1"]])
    w2 = np.concatenate([v["ffn_rw2"], v["ffn_sw2"]])
    bias1 = np.concatenate([v["ffn_rb1"], v["ffn_sb1"]])
    arrays = {
        "x": lay(v["attn_x"]), "wq": chunk(v["attn_W_q"]), "wkv": chunk(v["attn_W_kv"]), "woT": chunk(v["attn_W_o"].T),
        "rw": chunk(v["ffn_router_w"]), "rb": lay(v["ffn_router_b"]),
        "w1": lay(w1.reshape(EA, KD, P, HID).transpose(2, 0, 1, 3).reshape(P, -1)),
        "w2": lay(w2.reshape(EA, 2, HC, D).transpose(2, 0, 1, 3).reshape(HC, -1)),
        "b1": lay(bias1.reshape(EA, 2, HC).transpose(2, 0, 1).reshape(HC, -1)),
        "rb2": lay(v["ffn_rb2"]), "sb2": lay(v["ffn_sb2"]), **constants(),
    }
    nc = bacc.Bacc("TRN2", target_bir_lowering=False, num_devices=1)
    aps = {n: nc.dram_tensor("in_" + n, t.shape, mybir.dt.from_np(t.dtype), kind="ExternalInput").ap()
           for n, t in arrays.items()}
    out = nc.dram_tensor("out", (B, S, D), F32, kind="ExternalOutput").ap()
    build(nc, aps, out)
    r = run_bass_kernel_spmd(nc, [{"in_" + n: t for n, t in arrays.items()}], core_ids=[0])
    return r.results[0]["out"]
```

```python
import numpy as np
from contextlib import ExitStack

import concourse.bass as bass
from concourse import mybir

F32, F16, I32, U32 = mybir.dt.float32, mybir.dt.float16, mybir.dt.int32, mybir.dt.uint32

P = 128
B, S, D = 4, 512, 256
TOK = B * S
NT = TOK // P
TB = S // P
KD = D // P
HEADS = 16
HD = D // HEADS
NF = HD // 2
E = 32
NS = 2
EA = E + NS
HID = 176
HC = HID // 2
TOPK = 6
NBLK = P
EPS = 1e-5
SC = 16.0
LNCH = 3
GS = 2
NW = EA // GS
RING = 4
UN = 2 * RING
NST = 3
assert NBLK == TOK * TOPK // P + E and NBLK % UN == 0

BACK = 4
NWORD = 2 * (NBLK // UN)
WBLK, EBITS = (UN + BACK) // 2, 5
LOW = 3
assert E <= 2 ** EBITS and 2 * WBLK == UN + BACK
C_IOTA_E = 0
C_EDGE = C_IOTA_E + E
C_PIDX = C_EDGE + NT
C_TOKID = C_PIDX + 1
C_IDENT = C_TOKID + NT
C_HEADSUM = C_IDENT + P
C_PACK = C_HEADSUM + HEADS
C_ALL = C_PACK + 2 * NWORD
H_SLOT = 0
H_TRI = P
H_ONES = 2 * P
H_IDENT = 3 * P
H_ALL = 4 * P


def build(nc, a, out):
    ACT = mybir.ActivationFunctionType
    ALU = mybir.AluOpType
    AX = mybir.AxisListType.X

    ctx = ExitStack()
    with ctx:
        def sb(name, shape, dt):
            return ctx.enter_context(nc.sbuf_tensor(name, shape, dt))

        def sem(name):
            return ctx.enter_context(nc.semaphore(name))

        def cut(t, at, words, dt=F32, rows=P):
            v = t[0:rows, at:at + words]
            return v if dt == F32 else v.bitcast(dt)

        XR = sb("XR", [P, NT * D], F32)
        xn = XR[:, :].rearrange("p (t d) -> p t d", t=NT)
        prod32 = cut(XR, 0, LNCH * S).rearrange("p (c t) -> p c t", c=LNCH)
        h32s = cut(XR, LNCH * S, 2 * NS * S, rows=HC).rearrange("p (c t) -> p c t", c=2 * NS)
        TE = NT * E
        OH = cut(XR, 0, TOPK * TE // 2, F16).rearrange("p (k t e) -> p k t e", k=TOPK, t=NT)
        at = TOPK * TE // 2
        prb, dlog, pos, tmp = (cut(XR, at + i * TE, TE).rearrange("p (t e) -> p t e", t=NT) for i in range(4))
        yb = cut(XR, at + TE, RING * D).rearrange("p (r n) -> p r n", r=RING)
        at += 4 * TE
        mask = cut(XR, at, TE // 2, F16).rearrange("p (t e) -> p t e", t=NT)
        assert RING * D <= 3 * TE
        SR = sb("SR", [P, NT * D], F32)
        xs = cut(SR, 0, NT * D, F16).rearrange("p (t h d) -> p t h d", t=NT, h=2)
        xT_hi = cut(SR, 0, NT * D // 2, F16).rearrange("p (k t) -> p k t", k=KD)
        xT_lo = cut(SR, NT * D // 2, NT * D // 2, F16).rearrange("p (k t) -> p k t", k=KD)
        TR = sb("TR", [P, KD * TOK], F32)
        w_raw = [cut(TR, i * KD * D, KD * D).rearrange("p (k n) -> p k n", k=KD) for i in range(3)]
        f_mat = cut(TR, 3 * KD * D, KD * D).rearrange("p (k n) -> p k n", k=KD)
        g_mat = cut(TR, 4 * KD * D, KD * LNCH * P).rearrange("p (k n) -> p k n", k=KD)
        xT32 = TR[:, :].rearrange("p (k t) -> p k t", k=KD)
        xg = cut(TR, 0, RING * D, F16).rearrange("p (r c) -> p r c", r=RING)
        xgT = cut(TR, RING * D, RING * D, F16).rearrange("p (r c s) -> p r c s", r=RING, c=4)
        h32 = cut(TR, 2 * RING * D, RING * 2 * P, rows=HC).rearrange("p (r m s) -> p r m s", r=RING, m=2)
        h_hi = cut(TR, 2 * RING * D + 2 * RING * P, RING * P, F16, rows=HC).rearrange("p (r m s) -> p r m s", r=RING, m=2)
        h_lo = cut(TR, 2 * RING * D + 3 * RING * P, RING * P, F16, rows=HC).rearrange("p (r m s) -> p r m s", r=RING, m=2)
        work = [cut(TR, i * S, S) for i in range(6)]
        ones_s = cut(TR, 6 * S, S)
        W1N, W2N = EA * KD * HID, EA * 2 * D
        W1H = sb("W1H", [P, W1N // 2], F32)
        W1L = sb("W1L", [P, W1N // 2], F32)
        W2H = sb("W2H", [P, W2N // 2], F32)
        W2L = sb("W2L", [P, W2N // 2], F32)
        w1h, w1l = cut(W1H, 0, W1N // 2, F16), cut(W1L, 0, W1N // 2, F16)
        w2h, w2l = cut(W2H, 0, W2N // 2, F16, rows=HC), cut(W2L, 0, W2N // 2, F16, rows=HC)
        acc = cut(W1H, 0, NT * D).rearrange("p (t d) -> p t d", t=NT)
        q32 = cut(W1H, NT * D, 2 * S).rearrange("p (c t) -> p c t", c=2)
        rows = cut(W1L, 0, 2 * TOPK * D).rearrange("p (r k d) -> p r k d", r=2, k=TOPK)
        k32 = cut(W1L, 2 * TOPK * D, 2 * S).rearrange("p (c t) -> p c t", c=2)
        kc32 = cut(W1L, 2 * TOPK * D + 2 * S, 2 * S).rearrange("p (c t) -> p c t", c=2)
        hs_hi = cut(W2H, 0, NS * TOK, F16, rows=HC).rearrange("p (c t) -> p c t", c=2 * NS)
        hs_lo = cut(W2H, NS * TOK, NS * TOK, F16, rows=HC).rearrange("p (c t) -> p c t", c=2 * NS)
        p_hi = cut(W2L, 0, LNCH * TOK // 2, F16).rearrange("p (c t) -> p c t", c=LNCH)
        p_lo = cut(W2L, LNCH * TOK // 2, LNCH * TOK // 2, F16).rearrange("p (c t) -> p c t", c=LNCH)
        rvx = cut(W2L, LNCH * TOK, 2 * TB * P).rearrange("p (n c) -> p n c", n=2)
        assert NT * D + 2 * S <= E * KD * HID // 2 and 2 * TOPK * D + 4 * S <= E * KD * HID // 2
        assert 2 * NS * TOK <= E * D and LNCH * TOK + 2 * TB * P <= E * D
        G1, G2 = GS * KD * HID, GS * 2 * D
        GR = sb("GR", [P, NST * (G1 + G2)], F32)
        st1 = [cut(GR, r * (G1 + G2), G1) for r in range(NST)]
        st2 = [cut(GR, r * (G1 + G2) + G1, G2, rows=HC) for r in range(NST)]
        gT = [cut(GR, i * TOK // 2, TOK // 2, F16, rows=E + NS) for i in range(2)]
        b2p = [sb(f"b2{h}", [E + NS, D], F16) for h in "hl"]
        aw = [[sb(f"aw{n}{h}", [P, KD, D], F16) for h in "hl"] for n in "qk"]
        bw = [sb(f"bw{h}", [P, LNCH, D], F16) for h in "hl"]
        cf = sb("cf", [P, C_ALL], F32)
        ch = sb("ch", [P, H_ALL], F16)
        rw = sb("rw", [P, KD, E], F32)
        rb = sb("rb", [P, E], F32)
        b1 = sb("b1", [HC, EA * 2], F32)
        b1s = sb("b1s", [HC, EA * 2], F32)
        b2 = sb("b2", [E + NS, D], F32)
        stats = sb("stats", [P, NT, 6], F32)
        mv = sb("mv", [P, NT, 2], F32)
        std, rstd, t16a, t16b = (sb(n, [P, NT], F32) for n in ("std", "rstd", "t16a", "t16b"))
        gates = sb("gates", [P, NT, E], F32)
        m8 = sb("m8", [P, NT, 8], F32)
        i8 = sb("i8", [P, NT, 8], U32)
        i8f = sb("i8f", [P, NT, 8], F32)
        gate = sb("gate", [P, NT, TOPK], F32)
        cnt, nblk, cum, first = (sb(n, [P, E], F32) for n in ("cnt", "nblk", "cum", "first"))
        ones_e = sb("ones_e", [P, E], F32)
        posk = sb("posk", [P, TOPK, NT], F32)
        row_of = sb("row_of", [P, TOPK, NT], I32)
        slot_i = sb("slot_i", [P, 2, TOPK, NT], I32)
        slot_f = sb("slot_f", [P, 2, TOPK, NT], F32)
        NOH = 4
        oh_slot = sb("oh_slot", [P, NOH, P], F16)
        oh_blk = sb("oh_blk", [P, NOH, P], F16)
        token_of = sb("token_of", [P, NBLK], I32)
        ebc = sb("ebc", [P, 1], F32)
        parts_of = sb("parts_of", [1, 2, NWORD], I32)
        experts = sb("experts", [1, NWORD], I32)
        xg_idx = sb("xg_idx", [P, UN], I32)
        row_idx = sb("row_idx", [P, 2, TOPK], I32)
        NV = 2 * TB * HEADS
        sv, rv, rvi = (sb(n, [P, NV], F32) for n in ("sv", "rv", "rvi"))

        xs_dram = nc.dram_tensor("xs_dram", [TOK, 2 * D], F16, kind="Internal").ap()
        y_dram = nc.dram_tensor("y_dram", [NBLK * P, D], F32, kind="Internal").ap()

        ps = [ctx.enter_context(nc.psum_tensor(f"ps{i}", [P, 512], F32)) for i in range(8)]
        ps_x = [ps[i][:, 0:D].bitcast(F16) for i in (0, 1)]
        ps_h = [ps[i][0:HC, 0:2 * P] for i in (2, 3, 6, 7)]
        ps_y = [ps[i][:, 0:D] for i in (4, 5)]

        ident32, headsum = cf[:, C_IDENT:C_IDENT + P], cf[:, C_HEADSUM:C_PACK]
        slot_iota, tri, ones16, ident16 = (ch[:, i:i + P] for i in (H_SLOT, H_TRI, H_ONES, H_IDENT))

        s_x = [sem(f"s_x{g}") for g in range(B)]
        s_raw, s_const = sem("s_raw"), sem("s_const")
        s_w = [sem(f"s_w{r}") for r in range(NST)]
        s_wh, s_wl = sem("s_wh"), sem("s_wl")
        s_xs, s_xsd = sem("s_xs"), sem("s_xsd")
        s_d = sem("s_d")
        s_std, s_ln = sem("s_std"), sem("s_ln")
        s_ab, s_abs = sem("s_ab"), sem("s_abs")
        s_abl = sem("s_abl")
        s_tr, s_xt = sem("s_tr"), sem("s_xt")
        s_xth, s_xtl = sem("s_xth"), sem("s_xtl")
        s_log, s_dl, s_exp = sem("s_log"), sem("s_dl"), sem("s_exp")
        s_mask, s_cnt, s_gates = sem("s_mask"), sem("s_cnt"), sem("s_gates")
        s_oh, s_tab = sem("s_oh"), sem("s_tab")
        s_eb, s_ebr, s_lists = sem("s_eb"), sem("s_ebr"), sem("s_lists")
        s_bias = sem("s_bias")
        s_hold = sem("s_hold")
        s_gi = sem("s_gi")
        s_g = [sem(f"s_g{r}") for r in range(RING)]
        s_T, s_X, s_H, s_R, s_C, s_S, s_L, s_Y = (sem("s_" + n) for n in "TXHRCSLY")
        s_yd = [sem(f"s_yd{r}") for r in range(RING)]
        s_acc = sem("s_acc")
        s_ri = sem("s_ri")
        s_r = [sem(f"s_r{r}") for r in range(2)]
        s_sum = sem("s_sum")
        s_gt, s_gtc, s_gtl = sem("s_gt"), sem("s_gtc"), sem("s_gtl")
        s_sp, s_spc = sem("s_sp"), sem("s_spc")
        s_sq, s_nm, s_rt, s_nr = sem("s_sq"), sem("s_nm"), sem("s_rt"), sem("s_nr")
        s_rv, s_rx, s_ex = sem("s_rv"), sem("s_rx"), sem("s_ex")
        s_p32, s_ph, s_pl = sem("s_p32"), sem("s_ph"), sem("s_pl")
        s_sh, s_shr, s_shh, s_shl = sem("s_sh"), sem("s_shr"), sem("s_shh"), sem("s_shl")
        s_v = sem("s_v")
        s_o, s_fin = sem("s_o"), sem("s_fin")
        s_out = sem("s_out")

        S0, Y0 = 3, 5
        N_RAW, N_CONST = 5, 7

        def hold(eng, s, value):
            eng.wait_ge(s, value)
            eng.sem_inc(s_hold, 1)

        def after(eng, s, value, alone=True):
            if isinstance(value, int) and value <= 0:
                return
            if alone:
                hold(eng, s, value)
            else:
                eng.wait_ge(s, value)

        def weight_steps(eng, work, lo, hi):
            assert lo % NST == 0
            if hi // NST > lo // NST:
                with eng.Fori(lo // NST, hi // NST) as i:
                    for r in range(NST):
                        work(NST * i + r, r, i)
            for step in range(hi // NST * NST, hi):
                work(step, step % NST, step // NST)

        def pipeline(eng, stages, load=None):
            def steps(lo, hi):
                for s in range(lo, hi):
                    for lag, stage in stages:
                        if 0 <= s + lag < NBLK:
                            stage(0, s + lag)

            assert all(lag >= -BACK for lag, stage in stages)
            if load:
                load(0)
            steps(-BACK, UN)
            with eng.Fori(1, NBLK // UN - 1) as i:
                if load:
                    load(i)
                for s in range(UN):
                    for lag, stage in stages:
                        stage(i, s + lag)
            if load:
                load(NBLK // UN - 1)
            steps(NBLK - UN, NBLK + BACK)

        def experts_of(eng):
            expert = {}

            def load(i):
                for half in range(2):
                    word = eng.value_load(experts[0:1, bass.ds(2 * i + half, 1)])
                    for j in range(WBLK):
                        r = WBLK * half + j - BACK
                        expert[r] = expert[NBLK - UN + r] = (word >> (EBITS * j)) & (2 ** EBITS - 1)

            return expert, load

        with nc.Block() as block:

            @block.sync
            def _(eng):
                for dst, name in zip((*w_raw, f_mat, g_mat), ("wq", "wkv", "woT", "f_mat", "g_mat")):
                    eng.dma_start(dst, a[name]).then_inc(s_raw, 16)
                for g in range(B):
                    eng.dma_start(xn[:, g * TB:(g + 1) * TB, :],
                                  a["x"][g].rearrange("(t p) d -> p t d", p=P)).then_inc(s_x[g], 16)
                for dst, src in ((cf[:, :], a["cf"]), (ch[:, :], a["ch"]), (rw[:, :, :], a["rw"]),
                                 (rb[:, :], a["rb"].partition_broadcast(P)), (b1[:, :], a["b1"]),
                                 (b2[0:E, :], a["rb2"]), (b2[E:E + NS, :], a["sb2"])):
                    eng.dma_start(dst, src).then_inc(s_const, 16)

                def weights(step, r, turn):
                    if not isinstance(step, int) or step >= NST:
                        hold(eng, s_wl, 2 * (step - NST + 1))
                    eng.dma_start(st1[r], a["w1"][:, bass.ds(step * G1, G1)]).then_inc(s_w[r], 16)
                    eng.dma_start(st2[r], a["w2"][:, bass.ds(step * G2, G2)]).then_inc(s_w[r], 16)

                for step in range(NST):
                    weights(step, step, 0)
                eng.wait_ge(s_xs, NT)
                eng.dma_start(xs_dram.rearrange("(t p) c -> p t c", p=P),
                              xs.rearrange("p t h d -> p t (h d)")).then_inc(s_xsd, 16)
                weight_steps(eng, weights, NST, NW)
                with eng.Fori(0, NBLK // RING) as i:
                    for r in range(RING):
                        hold(eng, s_Y, RING * i + r + Y0 + 1)
                        eng.dma_start(y_dram[bass.ds((RING * i + r) * P, P), :], yb[:, r, :]).then_inc(s_yd[r], 16)
                eng.wait_ge(s_L, NBLK)
                eng.dma_start(acc, a["x"].rearrange("b (t p) d -> p (b t) d", p=P)).then_inc(s_acc, 16)
                with eng.Fori(0, NT) as t:
                    hold(eng, s_fin, t + 3)
                    eng.dma_start(out.rearrange("b s d -> (b s) d")[bass.ds(t * P, P), :],
                                  acc[:, bass.ds(t, 1), :].rearrange("p a d -> p (a d)")).then_inc(s_out, 16)
                eng.wait_ge(s_out, 16 * NT)

            @block.gpsimd
            def _(eng):
                def low(step, r, turn):
                    hold(eng, s_wh, 4 * step + 4)
                    eng.tensor_tensor(w1l[:, bass.ds(step * G1, G1)], st1[r], w1h[:, bass.ds(step * G1, G1)],
                                      ALU.subtract).then_inc(s_wl, 1)
                    eng.tensor_tensor(w2l[:, bass.ds(step * G2, G2)], st2[r], w2h[:, bass.ds(step * G2, G2)],
                                      ALU.subtract).then_inc(s_wl, 1)

                weight_steps(eng, low, 0, NW)
                for c in range(KD * B):
                    k, g = c // B, c % B
                    eng.wait_ge(s_xth, c + 1)
                    eng.tensor_tensor(xT_lo[:, k, g * S:(g + 1) * S], xT32[:, k, g * S:(g + 1) * S],
                                      xT_hi[:, k, g * S:(g + 1) * S], ALU.subtract).then_inc(s_xtl, 1)
                eng.wait_ge(s_lists, 2)
                eng.wait_ge(s_xsd, 16)
                eng.wait_ge(s_xtl, KD * B)
                with eng.Fori(0, NBLK // UN) as i:
                    for r in range(UN):
                        hold(eng, s_T, UN * i + r + 1)
                        if r % RING == 0:
                            eng.tensor_copy(xg_idx[:, r:r + RING], token_of[:, bass.ds(UN * i + r, RING)]).then_inc(s_gi, 1)
                            hold(eng, s_gi, (UN // RING) * i + r // RING + 1)
                        eng.indirect_dma_start(
                            out=xg[:, r % RING, :], out_offset=None, in_=xs_dram,
                            in_offset=bass.IndirectOffsetOnAxis(ap=xg_idx[:, r:r + 1], axis=0)).then_inc(s_g[r % RING], 16)
                for r in range(RING):
                    eng.wait_ge(s_yd[r], 16 * (NBLK // RING))
                eng.wait_ge(s_L, NBLK)
                with eng.Fori(0, NT // 2) as i:
                    for r in range(2):
                        hold(eng, s_sum, 2 * i + r + 1)
                        eng.tensor_copy(row_idx[:, r, :].unsqueeze(2), row_of[:, :, bass.ds(2 * i + r, 1)]).then_inc(s_ri, 1)
                        hold(eng, s_ri, 2 * i + r + 1)
                        for k in range(TOPK):
                            eng.indirect_dma_start(
                                out=rows[:, r, k, :], out_offset=None, in_=y_dram,
                                in_offset=bass.IndirectOffsetOnAxis(ap=row_idx[:, r, k:k + 1], axis=0)).then_inc(s_r[r], 16)

            @block.scalar
            def _(eng):
                eng.wait_ge(s_const, 16 * N_CONST)
                eng.activation(b1s[:, 0:2 * E], b1[:, 0:2 * E], ACT.Copy, scale=SC).then_inc(s_bias, 1)
                eng.activation(b1s[:, 2 * E:], b1[:, 2 * E:], ACT.Copy, scale=SC / NS).then_inc(s_bias, 1)
                eng.wait_ge(s_d, 1)
                def high(step, r, n):
                    hold(eng, s_w[r], 32 * (n + 1))
                    for st, w, g in ((st1, w1h, G1), (st2, w2h, G2)):
                        eng.activation(w[:, bass.ds(step * g, g)], st[r], ACT.Copy, scale=SC).then_inc(s_wh, 1)
                        eng.activation(st[r], st[r], ACT.Copy, scale=SC).then_inc(s_wh, 1)

                for c in range(2 * KD + LNCH):
                    w, k = (aw[c // KD], c % KD) if c < 2 * KD else (bw, c - 2 * KD)
                    eng.wait_ge(s_ab, c + 1)
                    eng.activation(w[0][:, k, :], ps[c][:, 0:D], ACT.Copy, scale=SC).then_inc(s_abs, 1)
                eng.wait_ge(s_d, 1)
                eng.activation(std[:, :], t16a[:, :], ACT.Sqrt).then_inc(s_std, 1)
                high(0, 0, 0)
                high(1, 1, 0)
                eng.wait_ge(s_abl, 2 * KD + LNCH)
                for c in range(KD * B):
                    k, g = c // B, c % B
                    eng.wait_ge(s_tr, c + 1)
                    eng.activation(xT32[:, k, g * S:(g + 1) * S], ps[c % 4][:, :], ACT.Copy).then_inc(s_xt, 1)
                high(2, 2, 0)
                eng.wait_ge(s_dl, 1)
                eng.wait_ge(s_xt, KD * B)
                eng.activation(prb, dlog, ACT.Exp).then_inc(s_exp, 1)
                eng.wait_ge(s_xsd, 16)
                for c in range(KD * B):
                    k, g = c // B, c % B
                    eng.activation(xT_hi[:, k, g * S:(g + 1) * S], xT32[:, k, g * S:(g + 1) * S], ACT.Copy).then_inc(s_xth, 1)

                weight_steps(eng, high, NST, NW)

                eng.wait_ge(s_bias, 2)
                eng.wait_ge(s_lists, 2)
                eng.wait_ge(s_xtl, KD * B)

                expert, load = experts_of(eng)

                def relu(i, r):
                    blk = UN * i + r
                    e = expert[r]
                    hold(eng, s_H, blk + 1)
                    for m in range(2):
                        eng.activation(h32[:, r % RING, m, :], ps_h[r % RING][:, m * P:(m + 1) * P], ACT.Relu,
                                       bias=b1s[:, bass.ds(2 * e + m, 1)], scale=1.0 / SC).then_inc(s_R, 1)

                def rows_out(i, r):
                    blk, slot, n = UN * i + r, r % RING, (UN // RING) * i + r // RING
                    after(eng, s_L, blk + 1)
                    after(eng, s_yd[slot], 16 * n)
                    eng.activation(yb[:, slot, :], ps_y[r % 2], ACT.Copy, scale=1.0 / (SC * SC)).then_inc(s_Y, 1)

                pipeline(eng, [(-3, rows_out), (0, relu)], load)

                eng.wait_ge(s_L, NBLK)
                eng.wait_ge(s_S, NBLK + S0)
                for r in range(RING):
                    eng.wait_ge(s_yd[r], 16 * (NBLK // RING))
                eng.activation(b2p[0][:, :], b2[:, :], ACT.Copy, scale=SC).then_inc(s_gtc, 1)
                for g in range(B):
                    eng.wait_ge(s_gt, g + 1)
                    eng.activation(gT[0][0:E, g * S:(g + 1) * S], ps[g][0:E, :], ACT.Copy, scale=SC).then_inc(s_gtc, 1)
                with eng.Fori(0, B) as b:
                    hold(eng, s_pl, LNCH * b + 1)
                    for c in range(4):
                        dst = (q32, k32)[c // 2][:, c % 2, :]
                        hold(eng, s_sp, 4 * b + c + 1)
                        eng.activation(dst, ps[c][:, :], ACT.Copy, scale=1.0 / (SC * SC)).then_inc(s_spc, 1)
                        hold(eng, s_spc, 4 * b + c + 1)
                        eng.activation(work[c], dst, ACT.Square).then_inc(s_sq, 1)
                    hold(eng, s_shl, 2 * NS * b + 1)
                    for c in range(2 * NS):
                        hold(eng, s_sh, 2 * NS * b + c + 1)
                        eng.activation(h32s[:, c, :], ps[6 + c % 2][0:HC, :], ACT.Relu,
                                       bias=b1s[:, 2 * E + c:2 * E + c + 1], scale=1.0 / (SC * NS)).then_inc(s_shr, 1)
                    hold(eng, s_nm, b + 1)
                    eng.activation(sv[:, :], ps[4][:, 0:NV], ACT.Sqrt).then_inc(s_rt, 1)
                    hold(eng, s_rv, b + 1)
                    for n in (1, 0):
                        eng.activation(rvx[:, n, :].rearrange("p (h f) -> p h f", f=NF),
                                       rvi[:, n * TB * HEADS:(n + 1) * TB * HEADS].unsqueeze(2).to_broadcast([P, TB * HEADS, NF]),
                                       ACT.Copy).then_inc(s_rx, 1)
                    for c in range(2 * NS):
                        hold(eng, s_shr, 2 * NS * b + c + 1)
                        eng.activation(hs_hi[:, c, bass.ds(b * S, S)], h32s[:, c, :], ACT.Copy).then_inc(s_shh, 1)
                    for c in range(LNCH):
                        hold(eng, s_p32, LNCH * b + c + 1)
                        eng.activation(p_hi[:, c, bass.ds(b * S, S)], prod32[:, c, :], ACT.Copy).then_inc(s_ph, 1)

            @block.vector
            def _(eng):
                n_d = [0]

                def own(ins):
                    ins.then_inc(s_d, 1)
                    n_d[0] += 1
                    eng.wait_ge(s_d, n_d[0])

                for t in range(NT):
                    eng.wait_ge(s_x[t // TB], 16)
                    last = eng.bn_stats(stats[:, t, :], xn[:, t, :])
                    last.then_inc(s_ln, 1)
                for t in range(NT):
                    eng.wait_ge(s_ln, t + 1)
                    eng.bn_aggr(mv[:, t, :], stats[:, t, :]).then_inc(s_ln, 1)
                eng.wait_ge(s_ln, 2 * NT)
                var = mv[:, :, 1]
                own(eng.tensor_scalar(t16a[:, :], var, EPS, None, ALU.add))
                eng.wait_ge(s_std, 1)
                own(eng.reciprocal(t16b[:, :], std[:, :]))
                own(eng.tensor_tensor(t16b[:, :], t16b[:, :], t16a[:, :], ALU.mult))
                own(eng.tensor_tensor(t16b[:, :], t16b[:, :], std[:, :], ALU.add))
                own(eng.reciprocal(rstd[:, :], t16b[:, :]))
                own(eng.tensor_scalar(rstd[:, :], rstd[:, :], 2.0 * SC, None, ALU.mult))
                n_ln = 2 * NT
                for t in range(NT):
                    eng.tensor_scalar(xn[:, t, :], xn[:, t, :], mv[:, t, 0:1], rstd[:, t:t + 1],
                                      ALU.subtract, ALU.mult).then_inc(s_ln, 1)
                for c in range(2 * KD + LNCH):
                    w, k = (aw[c // KD], c % KD) if c < 2 * KD else (bw, c - 2 * KD)
                    eng.wait_ge(s_abs, c + 1)
                    eng.scalar_tensor_tensor(w[1][:, k, :], ps[c][:, 0:D], SC, w[0][:, k, :],
                                             ALU.mult, ALU.subtract).then_inc(s_abl, 1)
                for g in range(B):
                    t = slice(g * TB, (g + 1) * TB)
                    eng.wait_ge(s_ln, n_ln + (g + 1) * TB)
                    own(eng.tensor_copy(xs[:, t, 0, :], xn[:, t, :]))
                    eng.tensor_tensor(xs[:, t, 1, :], xn[:, t, :], xs[:, t, 0, :], ALU.subtract).then_inc(s_xs, TB)

                eng.wait_ge(s_log, 1)
                eng.wait_ge(s_tr, KD * B)
                own(eng.scalar_tensor_tensor(dlog, ps[4][:, :].rearrange("p (t e) -> p t e", t=NT), 1.0 / SC,
                                             rb[:, :].unsqueeze(1).to_broadcast([P, NT, E]), ALU.mult, ALU.add))
                own(eng.tensor_reduce(t16a[:, :], dlog, AX, ALU.max))
                eng.tensor_tensor(dlog, dlog, t16a[:, :].unsqueeze(2).to_broadcast([P, NT, E]),
                                  ALU.subtract).then_inc(s_dl, 1)
                eng.wait_ge(s_exp, 1)
                for t in range(NT):
                    own(eng.max(m8[:, t, :], prb[:, t, :]))
                    ins = eng.max_index(i8[:, t, :], m8[:, t, :], prb[:, t, :])
                    if t < NT - 1:
                        ins.then_inc(s_ln, 1)
                    else:
                        ins.then_inc(s_ln, 1)
                eng.wait_ge(s_ln, 4 * NT)
                own(eng.tensor_copy(i8f[:, :, :], i8[:, :, :]))
                for k in range(TOPK):
                    eng.tensor_tensor(OH[:, k, :, :], cf[:, C_IOTA_E:C_IOTA_E + E].unsqueeze(1).to_broadcast([P, NT, E]),
                                      i8f[:, :, k:k + 1].to_broadcast([P, NT, E]), ALU.is_equal).then_inc(s_mask, 1)
                own(eng.memset(ones_e[:, :], 1.0))
                eng.wait_ge(s_cnt, 1)
                totals = ps[6][:, :].rearrange("p (t e) -> p t e", t=NT)
                own(eng.memset(tmp[:, 0, :], 0.0))
                for t in range(NT):
                    dst = tmp[:, t + 1, :] if t < NT - 1 else cnt[:, :]
                    own(eng.tensor_tensor(dst, totals[:, t, :], tmp[:, t, :], ALU.add))
                own(eng.tensor_tensor(pos.rearrange("p t e -> p (t e)").rearrange("p (e t) -> p e t", e=E),
                                      cnt[:, :].unsqueeze(2).to_broadcast([P, E, NT]),
                                      cf[:, C_EDGE:C_EDGE + NT].unsqueeze(1).to_broadcast([P, E, NT]), ALU.is_gt))
                own(eng.tensor_reduce(nblk[:, :], pos.rearrange("p t e -> p (t e)").rearrange("p (e t) -> p e t", e=E), AX, ALU.add))
                own(eng.tensor_tensor_scan(cum[:, :], ones_e[:, :], nblk[:, :], 0.0, ALU.mult, ALU.add))
                own(eng.tensor_tensor(first[:, :], cum[:, :], nblk[:, :], ALU.subtract))
                own(eng.scalar_tensor_tensor(pos, first[:, :].unsqueeze(1).to_broadcast([P, NT, E]), float(P), tmp,
                                             ALU.mult, ALU.add))
                own(eng.tensor_tensor(pos, pos, ps[5][:, :].rearrange("p (t e) -> p t e", t=NT), ALU.add))
                for k in range(TOPK):
                    own(eng.tensor_tensor(dlog, OH[:, k, :, :], pos, ALU.mult))
                    own(eng.tensor_reduce(posk[:, k, :], dlog, AX, ALU.add))
                own(eng.tensor_copy(row_of[:, :, :], posk[:, :, :]))
                own(eng.tensor_scalar(slot_i[:, 0, :, :], row_of[:, :, :], P - 1, None, ALU.bitwise_and))
                own(eng.tensor_scalar(slot_i[:, 1, :, :], row_of[:, :, :], 7, None, ALU.logical_shift_right))
                own(eng.tensor_copy(slot_f[:, :, :, :], slot_i[:, :, :, :]))
                j = 0
                for k in range(TOPK):
                    for t in range(NT):
                        if j >= NOH:
                            eng.wait_ge(s_tab, j - NOH + 1)
                        eng.tensor_scalar(oh_slot[:, j % NOH, :], slot_iota, slot_f[:, 0, k, t:t + 1], None,
                                          ALU.is_equal).then_inc(s_oh, 1)
                        eng.tensor_scalar(oh_blk[:, j % NOH, :], slot_iota, slot_f[:, 1, k, t:t + 1],
                                          cf[:, C_TOKID + t:C_TOKID + t + 1], ALU.is_equal, ALU.mult).then_inc(s_oh, 1)
                        j += 1
                own(eng.tensor_scalar(nblk[:, :], cum[:, :], cf[:, C_PIDX:C_PIDX + 1], None, ALU.is_le))
                own(eng.tensor_reduce(first[:, 0:1], nblk[:, :], AX, ALU.add))
                eng.tensor_scalar(ebc[:, :], first[:, 0:1], float(E - 1), None, ALU.min).then_inc(s_eb, 1)
                eng.wait_ge(s_tab, NT * TOPK)
                eng.tensor_copy(token_of[:, :], ps[7][:, 0:NBLK]).then_inc(s_lists, 1)
                eng.wait_ge(s_ebr, 1)
                own(eng.tensor_copy(parts_of[:, :, :], ps[6][0:1, 0:2 * NWORD].rearrange("p (h w) -> p h w", h=2)))
                own(eng.tensor_scalar(parts_of[:, 1, :], parts_of[:, 1, :], EBITS * LOW, None, ALU.logical_shift_left))
                eng.tensor_tensor(experts[:, :], parts_of[:, 0, :], parts_of[:, 1, :], ALU.bitwise_or).then_inc(s_lists, 1)

                def tokens_out(i, r):
                    blk = UN * i + r
                    eng.wait_ge(s_T, blk + RING + 1)
                    eng.tensor_copy(xgT[:, r % RING, :, :].rearrange("p c s -> p (c s)"), ps_x[r % 2]).then_inc(s_X, 1)

                def units_hi(i, r):
                    blk = UN * i + r
                    eng.wait_ge(s_R, 2 * blk + 2)
                    eng.tensor_copy(h_hi[:, r % RING, :, :], h32[:, r % RING, :, :]).then_inc(s_C, 1)

                def units_lo(i, r):
                    blk = UN * i + r
                    eng.wait_ge(s_C, blk + 1)
                    eng.tensor_tensor(h_lo[:, r % RING, :, :], h32[:, r % RING, :, :], h_hi[:, r % RING, :, :],
                                      ALU.subtract).then_inc(s_S, 1)

                eng.wait_ge(s_xtl, KD * B)
                pipeline(eng, [(-1, units_hi), (2, tokens_out), (-1, units_lo)])

                eng.wait_ge(s_L, NBLK)
                own(eng.tensor_reduce(t16a[:, :], m8[:, :, 0:TOPK], AX, ALU.add))
                own(eng.reciprocal(t16b[:, :], t16a[:, :]))
                own(eng.tensor_tensor(gate[:, :, :], m8[:, :, 0:TOPK], t16b[:, :].unsqueeze(2).to_broadcast([P, NT, TOPK]), ALU.mult))
                with nc.allow_low_precision(reason="sums of zeros and at most one 1"):
                    own(eng.tensor_reduce(mask, OH.rearrange("p k t e -> p t e k"), AX, ALU.add))
                own(eng.tensor_tensor(gates[:, :, :], prb, mask, ALU.mult))
                own(eng.tensor_tensor(gates[:, :, :], gates[:, :, :], t16b[:, :].unsqueeze(2).to_broadcast([P, NT, E]), ALU.mult))
                eng.sem_inc(s_gates, 1)
                eng.wait_ge(s_acc, 16)
                eng.memset(ones_s, 1.0).then_inc(s_gtl, 1)
                eng.memset(gT[0][E:E + NS, :], SC / NS).then_inc(s_gtl, 1)
                eng.memset(gT[1][E:E + NS, :], 0.0).then_inc(s_gtl, 1)
                eng.wait_ge(s_gtc, 1)
                eng.scalar_tensor_tensor(b2p[1][:, :], b2[:, :], SC, b2p[0][:, :], ALU.mult, ALU.subtract).then_inc(s_gtl, 1)
                for g in range(B):
                    eng.wait_ge(s_gtc, g + 2)
                    eng.scalar_tensor_tensor(gT[1][0:E, g * S:(g + 1) * S], ps[g][0:E, :], SC, gT[0][0:E, g * S:(g + 1) * S],
                                             ALU.mult, ALU.subtract).then_inc(s_gtl, 1)
                eng.wait_ge(s_gtl, 4 + B)
                NORMS, PRODUCTS = 3, 6
                PER = NORMS + PRODUCTS + TB * (TOPK - 1)

                def counted(b, start):
                    n = [start]

                    def mine(ins, now=True):
                        ins.then_inc(s_v, 1)
                        n[0] += 1
                        if now:
                            hold(eng, s_v, b * PER + n[0])
                    return n, mine

                def norms(b):
                    n, mine = counted(b, (TB - 1) * (TOPK - 1))
                    hold(eng, s_rt, b + 1)
                    mine(eng.reciprocal(rv[:, :], sv[:, :]))
                    mine(eng.tensor_tensor(rv[:, :], rv[:, :], ps[4][:, 0:NV], ALU.mult))
                    mine(eng.tensor_tensor(rv[:, :], rv[:, :], sv[:, :], ALU.add))
                    eng.reciprocal(rvi[:, :], rv[:, :]).then_inc(s_rv, 1)

                def attention(b):
                    n, mine = counted(b, NORMS + TB * (TOPK - 1))
                    hold(eng, s_ex, 2 * b + 1)
                    mine(eng.tensor_tensor(k32, k32, ps[5][:, :].unsqueeze(1).to_broadcast([P, 2, S]), ALU.mult))
                    hold(eng, s_ex, 2 * b + 2)
                    mine(eng.scalar_tensor_tensor(q32, q32, SC, ps[4][:, :].unsqueeze(1).to_broadcast([P, 2, S]),
                                                  ALU.mult, ALU.mult), now=False)
                    for c in range(2):
                        mine(eng.tensor_tensor_scan(kc32[:, c, :], ones_s, k32[:, c, :], 0.0, ALU.mult, ALU.add), now=(c == 1))
                    eng.sem_inc(s_nr, 1)
                    hold(eng, s_ph, LNCH * b + 1)
                    mine(eng.tensor_tensor(work[4], q32[:, 0, :], kc32[:, 1, :], ALU.mult), now=False)
                    mine(eng.tensor_tensor(work[5], q32[:, 1, :], kc32[:, 0, :], ALU.mult), now=False)
                    eng.tensor_tensor(prod32[:, 0, :], q32[:, 0, :], kc32[:, 0, :], ALU.mult).then_inc(s_p32, 1)
                    eng.tensor_tensor(prod32[:, 1, :], q32[:, 1, :], kc32[:, 1, :], ALU.mult).then_inc(s_p32, 1)
                    hold(eng, s_v, b * PER + n[0])
                    eng.tensor_tensor(prod32[:, 2, :], work[4], work[5], ALU.add).then_inc(s_p32, 1)
                    for c in range(2 * NS):
                        hold(eng, s_shh, 2 * NS * b + c + 1)
                        eng.tensor_tensor(hs_lo[:, c, bass.ds(b * S, S)], h32s[:, c, :], hs_hi[:, c, bass.ds(b * S, S)],
                                          ALU.subtract).then_inc(s_shl, 1)
                    for c in range(LNCH):
                        hold(eng, s_ph, LNCH * b + c + 2)
                        eng.tensor_tensor(p_lo[:, c, bass.ds(b * S, S)], prod32[:, c, :], p_hi[:, c, bass.ds(b * S, S)],
                                          ALU.subtract).then_inc(s_pl, 1)
                    assert n[0] == PER

                def tile(t):
                    return acc[:, bass.ds(t, 1), :].rearrange("p a d -> p (a d)")

                def sum_rows(b, tiles):
                    for tt in tiles:
                        t, r = TB * b + tt, tt % 2
                        hold(eng, s_r[r], 16 * TOPK * (TB // 2 * b + tt // 2 + 1))
                        for k in range(TOPK):
                            g = gate[:, bass.ds(t, 1), k:k + 1].rearrange("p a k -> p (a k)")
                            ins = eng.scalar_tensor_tensor(tile(t), rows[:, r, k, :], g, tile(t), ALU.mult, ALU.add)
                            if k < TOPK - 1:
                                ins.then_inc(s_v, 1)
                                hold(eng, s_v, b * PER + NORMS * (tt == TB - 1) + (TOPK - 1) * tt + k + 1)
                            else:
                                ins.then_inc(s_sum, 1)

                def finish(b):
                    for tt in range(TB):
                        t = TB * b + tt
                        hold(eng, s_o, t + 1)
                        hold(eng, s_sum, t + 3)
                        eng.scalar_tensor_tensor(tile(t), ps[4 + tt % 2][:, 0:D], 1.0 / (SC * SC), tile(t),
                                                 ALU.mult, ALU.add).then_inc(s_fin, 1)

                sum_rows(0, range(0, TB - 1))
                norms(0)
                sum_rows(0, range(TB - 1, TB))
                attention(0)
                with eng.Fori(1, B) as b:
                    sum_rows(b, range(0, TB - 1))
                    norms(b)
                    sum_rows(b, range(TB - 1, TB))
                    attention(b)
                    finish(b - 1)
                finish(B - 1)

            @block.tensor
            def _(eng):
                eng.sem_inc(s_S, S0)
                eng.sem_inc(s_Y, Y0)
                eng.sem_inc(s_T, RING)
                eng.sem_inc(s_sum, 2)
                eng.sem_inc(s_pl, 1)
                eng.sem_inc(s_fin, 2)
                eng.sem_inc(s_ph, 1)
                eng.sem_inc(s_shl, 1)

                eng.wait_ge(s_raw, 16 * N_RAW)
                for c in range(2 * KD + LNCH):
                    for k in range(KD):
                        if c < 2 * KD:
                            m = c % KD
                            ins = eng.matmul(ps[c][:, 0:D], w_raw[c // KD][:, k, m * P:(m + 1) * P], f_mat[:, k, :],
                                             start=(k == 0), stop=(k == KD - 1))
                        else:
                            m = c - 2 * KD
                            ins = eng.matmul(ps[c][:, 0:D], g_mat[:, k, m * P:(m + 1) * P], w_raw[2][:, k, :],
                                             start=(k == 0), stop=(k == KD - 1))
                    ins.then_inc(s_ab, 1)

                eng.wait_ge(s_const, 16 * N_CONST)
                eng.wait_ge(s_abl, 2 * KD + LNCH)
                for c in range(KD * B):
                    k, g = c // B, c % B
                    eng.wait_ge(s_ln, 2 * NT + (g + 1) * TB)
                    if c >= 4:
                        eng.wait_ge(s_xt, c - 3)
                    for tt in range(TB):
                        ins = eng.transpose(ps[c % 4][:, tt * P:(tt + 1) * P], xn[:, g * TB + tt, k * P:(k + 1) * P], ident32)
                    ins.then_inc(s_tr, 1)
                eng.wait_ge(s_xt, KD * B)
                for t in range(NT):
                    for k in range(KD):
                        ins = eng.matmul(ps[4][:, t * E:(t + 1) * E], xT32[:, k, t * P:(t + 1) * P], rw[:, k, :],
                                         start=(k == 0), stop=(k == KD - 1))
                ins.then_inc(s_log, 1)
                for k in range(TOPK):
                    eng.wait_ge(s_mask, k + 1)
                    flat = OH[:, k, :, :].rearrange("p t e -> p (t e)")
                    eng.matmul(ps[5][:, :], tri, flat, start=(k == 0), stop=(k == TOPK - 1))
                    ins = eng.matmul(ps[6][:, :], ones16, flat, start=(k == 0), stop=(k == TOPK - 1))
                ins.then_inc(s_cnt, 1)
                for j in range(TOPK * NT):
                    eng.wait_ge(s_oh, 2 * j + 2)
                    eng.matmul(ps[7][:, 0:P], oh_slot[:, j % NOH, :], oh_blk[:, j % NOH, :],
                               start=(j == 0), stop=(j == TOPK * NT - 1)).then_inc(s_tab, 1)
                eng.wait_ge(s_eb, 1)
                eng.matmul(ps[6][0:1, 0:2 * NWORD], ebc[:, :], cf[:, C_PACK:C_ALL], start=True, stop=True).then_inc(s_ebr, 1)

                def transposes(i, r):
                    eng.wait_ge(s_g[r % RING], 16 * ((UN // RING) * i + r // RING + 1))
                    for c in range(4):
                        ins = eng.transpose(ps_x[r % 2][:, c * P:(c + 1) * P], xg[:, r % RING, c * P:(c + 1) * P], ident16)
                    ins.then_inc(s_T, 1)

                expert, load = experts_of(eng)

                def layer1(i, r):
                    blk = UN * i + r
                    e = expert[r]
                    eng.wait_ge(s_X, blk + 1)
                    for m in range(2):
                        j = 0
                        for k in range(KD):
                            for w, x_part in ((w1h, k), (w1h, KD + k), (w1l, k)):
                                ins = eng.matmul(ps_h[r % RING][:, m * P:(m + 1) * P],
                                                 w[:, k * HID + m * HC:][:, bass.ds(e * (KD * HID), HC)],
                                                 xgT[:, r % RING, x_part, :], start=(j == 0), stop=(j == 3 * KD - 1))
                                j += 1
                                if m == 0 and j == 1 and not (isinstance(i, int) and blk < Y0):
                                    eng.wait_ge(s_Y, blk + 1)
                    ins.then_inc(s_H, 1)

                def layer2(i, r):
                    blk = UN * i + r
                    e = expert[r]
                    if isinstance(i, int) and blk >= NBLK - S0:
                        eng.wait_ge(s_Y, blk + S0 + 1)
                    eng.wait_ge(s_S, blk + S0 + 1)
                    j = 0
                    for m in range(2):
                        for h, w in ((h_hi, w2h), (h_hi, w2l), (h_lo, w2h)):
                            ins = eng.matmul(ps_y[r % 2], h[:, r % RING, m, :], w[:, m * D:][:, bass.ds(e * (2 * D), D)],
                                             start=(j == 0), stop=(j == 5))
                            j += 1
                    ins.then_inc(s_L, 1)

                eng.wait_ge(s_wl, 2 * NW)
                eng.wait_ge(s_lists, 2)
                pipeline(eng, [(0, layer1), (-3, layer2), (2, transposes)], load)

                eng.wait_ge(s_R, 2 * NBLK)
                eng.wait_ge(s_gates, 1)
                for g in range(B):
                    for tt in range(TB):
                        ins = eng.transpose(ps[g][0:E, tt * P:(tt + 1) * P], gates[:, g * TB + tt, :], ident32)
                    ins.then_inc(s_gt, 1)
                eng.wait_ge(s_gtl, 4 + B)
                eng.wait_ge(s_Y, NBLK + Y0)

                def stage1(b):
                    for c in range(4):
                        if not (isinstance(b, int) and b == 0):
                            eng.wait_ge(s_spc, 4 * b - 4 + c + 1)
                        j = 0
                        w, m = aw[c // 2], c % 2
                        for k in range(KD):
                            for wp, xp in ((w[0], xT_hi), (w[0], xT_lo), (w[1], xT_hi)):
                                ins = eng.matmul(ps[c][:, :], wp[:, k, m * P:(m + 1) * P], xp[:, k, bass.ds(b * S, S)],
                                                 start=(j == 0), stop=(j == 3 * KD - 1))
                                j += 1
                        ins.then_inc(s_sp, 1)
                    for c in range(2 * NS):
                        if not (isinstance(b, int) and b == 0 and c < 2):
                            eng.wait_ge(s_shr, 2 * NS * b + c - 1)
                        j = 0
                        at = (E + c // 2) * KD * HID + (c % 2) * HC
                        for k in range(KD):
                            for wp, xp in ((w1h, xT_hi), (w1h, xT_lo), (w1l, xT_hi)):
                                ins = eng.matmul(ps[6 + c % 2][0:HC, :], wp[:, at + k * HID:at + k * HID + HC],
                                                 xp[:, k, bass.ds(b * S, S)], start=(j == 0), stop=(j == 3 * KD - 1))
                                j += 1
                        ins.then_inc(s_sh, 1)
                    eng.wait_ge(s_sq, 4 * b + 4)
                    if not isinstance(b, int):
                        eng.wait_ge(s_nr, b)
                        eng.wait_ge(s_fin, TB * (b - 1) + 2)
                    for n in range(2):
                        for tt in range(TB):
                            at = (n * TB + tt) * HEADS
                            for c in range(2):
                                ins = eng.matmul(ps[4][:, at:at + HEADS], work[2 * n + c][:, tt * P:(tt + 1) * P], headsum,
                                                 start=(c == 0), stop=(c == 1))
                    ins.then_inc(s_nm, 1)
                    for j, n in enumerate((1, 0)):
                        eng.wait_ge(s_rx, 2 * b + j + 1)
                        for tt in range(TB):
                            ins = eng.transpose(ps[4 + n][:, tt * P:(tt + 1) * P], rvx[:, n, tt * P:(tt + 1) * P], ident32)
                        ins.then_inc(s_ex, 1)

                def stage2(b, read):
                    eng.wait_ge(s_pl, LNCH * b + LNCH + 1)
                    eng.wait_ge(s_shl, 2 * NS * b + 2 * NS + 1)
                    eng.wait_ge(s_nr, read)
                    for tt in range(TB):
                        t = TB * b + tt
                        eng.wait_ge(s_fin, t + 1)
                        tok = bass.ds(t * P, P)
                        parts = [(p_, w[:, c, :], c) for c in range(LNCH) for p_, w in ((p_hi, bw[0]), (p_hi, bw[1]), (p_lo, bw[0]))]
                        for c in range(2 * NS):
                            at = (2 * E + c) * D
                            parts += [(h_, w[:, at:at + D], c) for h_, w in ((hs_hi, w2h), (hs_hi, w2l), (hs_lo, w2h))]
                        parts += [(g_.unsqueeze(1), b_[:, :], 0) for g_, b_ in ((gT[0], b2p[0]), (gT[0], b2p[1]), (gT[1], b2p[0]))]
                        for j, (lhs, rhs, c) in enumerate(parts):
                            ins = eng.matmul(ps[4 + tt % 2][:, 0:D], lhs[:, c, tok], rhs, start=(j == 0), stop=(j == len(parts) - 1))
                        ins.then_inc(s_o, 1)

                stage1(0)
                with eng.Fori(1, B) as b:
                    stage1(b)
                    stage2(b - 1, b + 1)
                stage2(B - 1, B)


def constants():
    cf = np.zeros((P, C_ALL), np.float32)
    p = np.arange(P)
    cf[:, C_IOTA_E:C_IOTA_E + E] = np.arange(E)
    cf[:, C_EDGE:C_EDGE + NT] = np.arange(NT) * P
    cf[:, C_PIDX] = p
    cf[:, C_TOKID:C_TOKID + NT] = np.arange(NT)[None, :] * P + p[:, None]
    cf[:, C_IDENT:C_IDENT + P] = np.eye(P)
    cf[:, C_HEADSUM:C_PACK] = (p[:, None] // NF) == np.arange(HEADS)[None, :]
    for w in range(NWORD):
        for j in range(WBLK):
            blk = UN * (w // 2) - BACK + WBLK * (w % 2) + j
            if blk >= 0:
                cf[blk, C_PACK + (j >= LOW) * NWORD + w] = 2 ** (EBITS * (j % LOW))
    ch = np.zeros((P, H_ALL), np.float16)
    ch[:, H_SLOT:H_SLOT + P] = p
    ch[:, H_TRI:H_TRI + P] = p[:, None] < p[None, :]
    ch[:, H_ONES:H_ONES + P] = 1
    ch[:, H_IDENT:H_IDENT + P] = np.eye(P)
    i, f = np.arange(HD)[:, None], np.arange(NF)[None, :]
    ang = 2 * np.pi * i * f / HD
    alt = (-1.0) ** np.arange(HD)
    re = np.sqrt(2.0 / HD) * np.cos(ang)
    im = -np.sqrt(2.0 / HD) * np.sin(ang)
    re[:, 0] = 1 / np.sqrt(HD)
    im[:, 0] = alt / np.sqrt(HD)
    rr, ii, ri = np.cos(ang) / HD, -np.cos(ang) / HD, -np.sin(ang) / HD
    ii[:, 0] = alt / HD
    ri[:, 0] = 0
    fm = np.zeros((HEADS, HD, 2, HEADS, NF))
    gm = np.zeros((HEADS, HD, LNCH, HEADS, NF))
    for h in range(HEADS):
        for c, m in enumerate((re, im)):
            fm[h, :, c, h, :] = m
        for c, m in enumerate((rr, ii, ri)):
            gm[h, :, c, h, :] = 4 * m
    chunk = lambda m: np.ascontiguousarray(m.reshape(KD, P, -1).transpose(1, 0, 2).astype(np.float32))
    return {"cf": cf, "ch": ch, "f_mat": chunk(fm), "g_mat": chunk(gm)}


def kernel(**inputs):
    import concourse.bacc as bacc
    from concourse.bass_utils import run_bass_kernel_spmd

    v = {n.replace("L0_", ""): np.asarray(t) for n, t in inputs.items()}
    lay = np.ascontiguousarray
    chunk = lambda m: lay(m.reshape(KD, P, -1).transpose(1, 0, 2))
    w1 = np.concatenate([v["ffn_rw1"], v["ffn_sw1"]])
    w2 = np.concatenate([v["ffn_rw2"], v["ffn_sw2"]])
    bias1 = np.concatenate([v["ffn_rb1"], v["ffn_sb1"]])
    arrays = {
        "x": lay(v["attn_x"]), "wq": chunk(v["attn_W_q"]), "wkv": chunk(v["attn_W_kv"]), "woT": chunk(v["attn_W_o"].T),
        "rw": chunk(v["ffn_router_w"]), "rb": lay(v["ffn_router_b"]),
        "w1": lay(w1.reshape(EA, KD, P, HID).transpose(2, 0, 1, 3).reshape(P, -1)),
        "w2": lay(w2.reshape(EA, 2, HC, D).transpose(2, 0, 1, 3).reshape(HC, -1)),
        "b1": lay(bias1.reshape(EA, 2, HC).transpose(2, 0, 1).reshape(HC, -1)),
        "rb2": lay(v["ffn_rb2"]), "sb2": lay(v["ffn_sb2"]), **constants(),
    }
    nc = bacc.Bacc("TRN2", target_bir_lowering=False, num_devices=1)
    aps = {n: nc.dram_tensor("in_" + n, t.shape, mybir.dt.from_np(t.dtype), kind="ExternalInput").ap()
           for n, t in arrays.items()}
    out = nc.dram_tensor("out", (B, S, D), F32, kind="ExternalOutput").ap()
    build(nc, aps, out)
    r = run_bass_kernel_spmd(nc, [{"in_" + n: t for n, t in arrays.items()}], core_ids=[0])
    return r.results[0]["out"]
```

```python
import numpy as np
from contextlib import ExitStack

import concourse.bass as bass
from concourse import mybir

F32, F16, I32, U32 = mybir.dt.float32, mybir.dt.float16, mybir.dt.int32, mybir.dt.uint32

P = 128
B, S, D = 4, 512, 256
TOK = B * S
NT = TOK // P
TB = S // P
KD = D // P
HEADS = 16
HD = D // HEADS
NF = HD // 2
E = 32
NS = 2
EA = E + NS
HID = 176
HC = HID // 2
SHC = [min(P, NS * HID - at) for at in range(0, NS * HID, P)]
SH = len(SHC)
TOPK = 6
NBLK = P
EPS = 1e-5
SC = 16.0
NPROD = 3
GS = 2
NW = EA // GS
assert GS == NS and E % GS == 0
RING = 4
UN = 2 * RING
NST = 3
ROWS = 4
assert NBLK == TOK * TOPK // P + E and NBLK % UN == 0

BACK = 4
NWORD = 2 * (NBLK // UN)
WBLK, EBITS = (UN + BACK) // 2, 5
LOW = 3
assert E <= 2 ** EBITS and 2 * WBLK == UN + BACK
C_IOTA_E = 0
C_EDGE = C_IOTA_E + E
C_PIDX = C_EDGE + NT
C_TOKID = C_PIDX + 1
C_IDENT = C_TOKID + NT
C_HEADSUM = C_IDENT + P
C_PACK = C_HEADSUM + HEADS
C_ALL = C_PACK + 2 * NWORD
H_TRI = 0
H_ONES = P
H_IDENT = 2 * P
H_COUNT = 3 * P
H_ALL = H_COUNT + P * TOPK


def build(nc, a, out):
    ACT = mybir.ActivationFunctionType
    ALU = mybir.AluOpType
    AX = mybir.AxisListType.X

    ctx = ExitStack()
    with ctx:
        def sb(name, shape, dt):
            return ctx.enter_context(nc.sbuf_tensor(name, shape, dt))

        def sem(name):
            return ctx.enter_context(nc.semaphore(name))

        def cut(t, at, words, dt=F32, rows=P):
            v = t[0:rows, at:at + words]
            return v if dt == F32 else v.bitcast(dt)

        XR = sb("XR", [P, NT * D], F32)
        xn = XR[:, :].rearrange("p (t d) -> p t d", t=NT)
        prod32 = cut(XR, 0, NPROD * S).rearrange("p (c t) -> p c t", c=NPROD)
        h32s = cut(XR, NPROD * S, SH * S).rearrange("p (c t) -> p c t", c=SH)
        TE = NT * E
        OH = cut(XR, 0, TOPK * TE // 2, F16).rearrange("p (k t e) -> p k t e", k=TOPK, t=NT)
        at = TOPK * TE // 2
        prb, dlog, pos, tmp = (cut(XR, at + i * TE, TE).rearrange("p (t e) -> p t e", t=NT) for i in range(4))
        yb = cut(XR, at + TE, RING * D).rearrange("p (r n) -> p r n", r=RING)
        oh_slot, oh_blk = (cut(XR, at + TE + i * P * TOPK, P * TOPK, F16).rearrange("p (r s k) -> p r s k", r=2, k=TOPK)
                           for i in range(2))
        assert 2 * P * TOPK <= 3 * TE
        at += 4 * TE
        mask = cut(XR, at, TE // 2, F16).rearrange("p (t e) -> p t e", t=NT)
        assert RING * D <= 3 * TE
        SR = sb("SR", [P, NT * D], F32)
        xs = cut(SR, 0, NT * D, F16).rearrange("p (t h d) -> p t h d", t=NT, h=2)
        xT_hi = cut(SR, 0, NT * D // 2, F16).rearrange("p (k t) -> p k t", k=KD)
        xT_lo = cut(SR, NT * D // 2, NT * D // 2, F16).rearrange("p (k t) -> p k t", k=KD)
        TR = sb("TR", [P, KD * TOK], F32)
        w_raw = [cut(TR, i * KD * D, KD * D).rearrange("p (k n) -> p k n", k=KD) for i in range(3)]
        f_mat = cut(TR, 3 * KD * D, KD * D).rearrange("p (k n) -> p k n", k=KD)
        g_mat = cut(TR, 4 * KD * D, KD * NPROD * P).rearrange("p (k n) -> p k n", k=KD)
        xT32 = TR[:, :].rearrange("p (k t) -> p k t", k=KD)
        xg = cut(TR, 0, RING * D, F16).rearrange("p (r c) -> p r c", r=RING)
        xgT = cut(TR, RING * D, RING * D, F16).rearrange("p (r c s) -> p r c s", r=RING, c=4)
        h32 = cut(TR, 2 * RING * D, RING * 2 * P, rows=HC).rearrange("p (r m s) -> p r m s", r=RING, m=2)
        h_hi = cut(TR, 2 * RING * D + 2 * RING * P, RING * P, F16, rows=HC).rearrange("p (r m s) -> p r m s", r=RING, m=2)
        h_lo = cut(TR, 2 * RING * D + 3 * RING * P, RING * P, F16, rows=HC).rearrange("p (r m s) -> p r m s", r=RING, m=2)
        work = [cut(TR, i * S, S) for i in range(6)]
        kn32 = cut(TR, 4 * S, 2 * S).rearrange("p (c t) -> p c t", c=2)
        W1N, W2N = EA * KD * HID, EA * 2 * D
        W1H = sb("W1H", [P, W1N // 2], F32)
        W1L = sb("W1L", [P, W1N // 2], F32)
        W2H = sb("W2H", [P, W2N // 2], F32)
        W2L = sb("W2L", [P, W2N // 2], F32)
        w1h, w1l = cut(W1H, 0, W1N // 2, F16), cut(W1L, 0, W1N // 2, F16)
        w2h, w2l = cut(W2H, 0, W2N // 2, F16, rows=HC), cut(W2L, 0, W2N // 2, F16, rows=HC)
        w1sh, w1sl = (w[:, E * KD * HID:].rearrange("p (k h) -> p k h", k=KD) for w in (w1h, w1l))
        w2sh, w2sl = (cut(w, E * D, SH * D // 2, F16) for w in (W2H, W2L))
        acc = cut(W1H, 0, NT * D).rearrange("p (t d) -> p t d", t=NT)
        q32 = cut(W1H, NT * D, 2 * S).rearrange("p (c t) -> p c t", c=2)
        k32 = cut(W1L, 2 * TOPK * D, 2 * S).rearrange("p (c t) -> p c t", c=2)
        kc32 = cut(W1L, 2 * TOPK * D + 2 * S, 2 * S).rearrange("p (c t) -> p c t", c=2)
        hs_hi, hs_lo = (cut(W2H, i * SH * TOK // 2, SH * TOK // 2, F16).rearrange("p (c t) -> p c t", c=SH) for i in (0, 1))
        p_hi = cut(W2L, 0, NPROD * TOK // 2, F16).rearrange("p (c t) -> p c t", c=NPROD)
        p_lo = cut(W2L, NPROD * TOK // 2, NPROD * TOK // 2, F16).rearrange("p (c t) -> p c t", c=NPROD)
        rvx = cut(W2L, NPROD * TOK, 2 * TB * P).rearrange("p (n c) -> p n c", n=2)
        qn32 = cut(W2L, NPROD * TOK + 2 * TB * P, 2 * S).rearrange("p (c t) -> p c t", c=2)
        assert NT * D + 2 * S <= E * KD * HID // 2 and 2 * TOPK * D + 4 * S <= E * KD * HID // 2
        assert SH * TOK <= E * D and NPROD * TOK + 2 * TB * P + 2 * S <= E * D
        G1, G2 = GS * KD * HID, GS * 2 * D
        GR = sb("GR", [P, NST * (G1 + G2)], F32)
        st1 = [cut(GR, r * (G1 + G2), G1) for r in range(NST)]
        st2 = [cut(GR, r * (G1 + G2) + G1, G2, rows=HC) for r in range(NST)]
        LASTBUF = (NST - 1) * (G1 + G2)
        gT = [cut(GR, at, TOK // 2, F16, rows=E + NS) for at in (LASTBUF, 0)]
        ones_s = cut(GR, LASTBUF + TOK // 2, S)
        assert NW % NST and LASTBUF + TOK // 2 + S <= NST * (G1 + G2)
        places = [(W1L, k * D) for k in range(2 * TOPK)] + [(GR, TOK // 2 + k * D) for k in range(TOPK)]
        places += [(TR, 6 * S + k * D) for k in range(4)] + [(W1H, NT * D + 2 * S + k * D) for k in range(2)]
        assert TOK // 2 + TOPK * D <= LASTBUF and 6 * S + 4 * D <= KD * TOK
        assert NT * D + 2 * S + 2 * D <= E * KD * HID // 2
        rows = [[cut(*places[TOPK * r + k], D) for k in range(TOPK)] for r in range(ROWS)]
        b2p = [sb(f"b2{h}", [E + NS, D], F16) for h in "hl"]
        aw = [[sb(f"aw{n}{h}", [P, KD, D], F16) for h in "hl"] for n in "qk"]
        bw = [sb(f"bw{h}", [P, NPROD, D], F16) for h in "hl"]
        cf = sb("cf", [P, C_ALL], F32)
        ch = sb("ch", [P, H_ALL], F16)
        rw = sb("rw", [P, KD, E], F32)
        rb = sb("rb", [P, E], F32)
        b1, b1s = (sb(n, [HC, E * 2], F32) for n in ("b1", "b1s"))
        b1sh, b1shs = (sb(n, [P, SH], F32) for n in ("b1sh", "b1shs"))
        b2 = sb("b2", [E + NS, D], F32)
        stats = sb("stats", [P, NT, 6], F32)
        mv = sb("mv", [P, NT, 2], F32)
        std, rstd, t16a, t16b = (sb(n, [P, NT], F32) for n in ("std", "rstd", "t16a", "t16b"))
        gates = sb("gates", [P, NT, E], F32)
        m8 = sb("m8", [P, NT, 8], F32)
        i8 = sb("i8", [P, NT, 8], U32)
        i8f = sb("i8f", [P, NT, 8], F32)
        gate = sb("gate", [P, NT, TOPK], F32)
        cnt, nblk, cum, first = (sb(n, [P, E], F32) for n in ("cnt", "nblk", "cum", "first"))
        ones_e = sb("ones_e", [P, E], F32)
        posk = sb("posk", [P, TOPK, NT], F32)
        row_of = sb("row_of", [P, TOPK, NT], I32)
        slot_i = sb("slot_i", [P, 2, TOPK, NT], I32)
        slot_f = sb("slot_f", [P, 2, NT, TOPK], F16)
        token_of = sb("token_of", [P, NBLK], I32)
        ebc = sb("ebc", [P, 1], F32)
        parts_of = sb("parts_of", [1, 2, NWORD], I32)
        experts = sb("experts", [1, NWORD], I32)
        xg_idx = sb("xg_idx", [P, UN], I32)
        row_idx = sb("row_idx", [P, ROWS, TOPK], I32)
        NV = 2 * TB * HEADS
        sv, rv, rvi = (sb(n, [P, NV], F32) for n in ("sv", "rv", "rvi"))

        xs_dram = nc.dram_tensor("xs_dram", [TOK, 2 * D], F16, kind="Internal").ap()
        y_dram = nc.dram_tensor("y_dram", [NBLK * P, D], F32, kind="Internal").ap()

        ps = [ctx.enter_context(nc.psum_tensor(f"ps{i}", [P, 512], F32)) for i in range(8)]
        ps_x = [ps[i][:, 0:D].bitcast(F16) for i in (0, 1)]
        ps_h = [ps[i][0:HC, 0:2 * P] for i in (2, 3, 6, 7)]
        ps_y = [ps[i][:, 0:D] for i in (4, 5)]

        ident32, headsum = cf[:, C_IDENT:C_IDENT + P], cf[:, C_HEADSUM:C_PACK]
        tri, ones16, ident16 = (ch[:, i:i + P] for i in (H_TRI, H_ONES, H_IDENT))
        counting = ch[:, H_COUNT:H_ALL].rearrange("p (s k) -> p s k", k=TOPK)

        s_x = [sem(f"s_x{g}") for g in range(B)]
        s_raw, s_const = sem("s_raw"), sem("s_const")
        s_w = [sem(f"s_w{r}") for r in range(NST)]
        s_wh, s_wl = sem("s_wh"), sem("s_wl")
        s_xs, s_xsd = sem("s_xs"), sem("s_xsd")
        s_d = sem("s_d")
        s_std, s_ln = sem("s_std"), sem("s_ln")
        s_ab, s_abs = sem("s_ab"), sem("s_abs")
        s_abl = sem("s_abl")
        s_tr, s_xt = sem("s_tr"), sem("s_xt")
        s_xth, s_xtl = sem("s_xth"), sem("s_xtl")
        s_log, s_dl, s_exp = sem("s_log"), sem("s_dl"), sem("s_exp")
        s_mask, s_cnt, s_gates = sem("s_mask"), sem("s_cnt"), sem("s_gates")
        s_oh, s_tab = sem("s_oh"), sem("s_tab")
        s_eb, s_ebr = sem("s_eb"), sem("s_ebr")
        s_lists = sem("s_lists")
        s_bias = sem("s_bias")
        s_hold = sem("s_hold")
        s_gi = sem("s_gi")
        s_g = [sem(f"s_g{r}") for r in range(RING)]
        s_T, s_X, s_H, s_R, s_C, s_S, s_L, s_Y = (sem("s_" + n) for n in "TXHRCSLY")
        s_yd = [sem(f"s_yd{r}") for r in range(RING)]
        s_acc = sem("s_acc")
        s_ri = sem("s_ri")
        s_r = [sem(f"s_r{r}") for r in range(ROWS)]
        s_sum = sem("s_sum")
        s_gt, s_gtc, s_gtl = sem("s_gt"), sem("s_gtc"), sem("s_gtl")
        s_sp, s_spc = sem("s_sp"), sem("s_spc")
        s_sq, s_nm, s_rt = sem("s_sq"), sem("s_nm"), sem("s_rt")
        s_rv, s_rx, s_ex = sem("s_rv"), sem("s_rx"), sem("s_ex")
        s_p32, s_ph, s_pl = sem("s_p32"), sem("s_ph"), sem("s_pl")
        s_sh, s_shr, s_shh, s_shl = sem("s_sh"), sem("s_shr"), sem("s_shh"), sem("s_shl")
        s_v = sem("s_v")
        s_o = sem("s_o")
        s_out = sem("s_out")

        S0, Y0 = 3, 5
        STEPS = 9
        LATE, REST = 2, (1, 1, 2, 3)
        ADDITIONS = []
        for tt in range(TB):
            ADDITIONS += [("rows", tt, k) for k in range(TOPK)] + [("rest", f) for f in range(TB) if REST[f] == tt]
        TURN = len(ADDITIONS)
        START = 7
        CREDIT = TURN + ADDITIONS.index(("rows", TB - LATE, 0))
        assert ROWS == TB and LATE < TB

        def added(b, *addition):
            return TURN * (b + 2) + ADDITIONS.index(addition) + 1

        def rows_added(b, tt):
            return added(b - (tt < LATE), "rows", (tt - LATE) % TB, TOPK - 1)

        N_RAW, N_CONST = 5, 8

        def hold(eng, s, value):
            eng.wait_ge(s, value)
            eng.sem_inc(s_hold, 1)

        def after(eng, s, value, alone=True):
            if isinstance(value, int) and value <= 0:
                return
            if alone:
                hold(eng, s, value)
            else:
                eng.wait_ge(s, value)

        def second_weights(step, r):
            if isinstance(step, int) and step == NW - 1:
                return cut(GR, r * (G1 + G2) + G1, SH * D), w2sh, w2sl
            at = bass.ds(step * G2, G2)
            return st2[r], w2h[:, at], w2l[:, at]

        def weight_steps(eng, work, lo, hi):
            assert lo % NST == 0
            if hi // NST > lo // NST:
                with eng.Fori(lo // NST, hi // NST) as i:
                    for r in range(NST):
                        work(NST * i + r, r, i)
            for step in range(hi // NST * NST, hi):
                work(step, step % NST, step // NST)

        def pipeline(eng, stages, load=None):
            def steps(lo, hi):
                for s in range(lo, hi):
                    for lag, stage in stages:
                        if 0 <= s + lag < NBLK:
                            stage(0, s + lag)

            assert all(lag >= -BACK for lag, stage in stages)
            if load:
                load(0)
            steps(-BACK, UN)
            with eng.Fori(1, NBLK // UN - 1) as i:
                if load:
                    load(i)
                for s in range(UN):
                    for lag, stage in stages:
                        stage(i, s + lag)
            if load:
                load(NBLK // UN - 1)
            steps(NBLK - UN, NBLK + BACK)

        def experts_of(eng):
            expert = {}

            def load(i):
                for half in range(2):
                    word = eng.value_load(experts[0:1, bass.ds(2 * i + half, 1)])
                    for j in range(WBLK):
                        r = WBLK * half + j - BACK
                        expert[r] = expert[NBLK - UN + r] = (word >> (EBITS * j)) & (2 ** EBITS - 1)

            return expert, load

        with nc.Block() as block:

            @block.sync
            def _(eng):
                for dst, name in zip((*w_raw, f_mat, g_mat), ("wq", "wkv", "woT", "f_mat", "g_mat")):
                    eng.dma_start(dst, a[name]).then_inc(s_raw, 16)
                for g in range(B):
                    eng.dma_start(xn[:, g * TB:(g + 1) * TB, :],
                                  a["x"][g].rearrange("(t p) d -> p t d", p=P)).then_inc(s_x[g], 16)
                for dst, src in ((cf[:, :], a["cf"]), (ch[:, :], a["ch"]), (rw[:, :, :], a["rw"]),
                                 (rb[:, :], a["rb"].partition_broadcast(P)), (b1[:, :], a["b1"]), (b1sh[:, :], a["b1s"]),
                                 (b2[0:E, :], a["rb2"]), (b2[E:E + NS, :], a["sb2"])):
                    eng.dma_start(dst, src).then_inc(s_const, 16)

                def weights(step, r, turn):
                    if not isinstance(step, int) or step >= NST:
                        hold(eng, s_wl, 2 * (step - NST + 1))
                    eng.dma_start(st1[r], a["w1"][:, bass.ds(step * G1, G1)]).then_inc(s_w[r], 16)
                    last = isinstance(step, int) and step == NW - 1
                    eng.dma_start(second_weights(step, r)[0],
                                  a["w2s"] if last else a["w2"][:, bass.ds(step * G2, G2)]).then_inc(s_w[r], 16)

                for step in range(NST):
                    weights(step, step, 0)
                for step in range(NST, 2 * NST):
                    if step == 2 * NST - 1:
                        eng.wait_ge(s_xs, NT)
                        eng.dma_start(xs_dram.rearrange("(t p) c -> p t c", p=P),
                                      xs.rearrange("p t h d -> p t (h d)")).then_inc(s_xsd, 16)
                    weights(step, step % NST, 1)
                weight_steps(eng, weights, 2 * NST, NW)
                with eng.Fori(0, NBLK // RING) as i:
                    for r in range(RING):
                        hold(eng, s_Y, RING * i + r + Y0 + 1)
                        eng.dma_start(y_dram[bass.ds((RING * i + r) * P, P), :], yb[:, r, :]).then_inc(s_yd[r], 16)
                eng.wait_ge(s_L, NBLK)
                eng.dma_start(acc, a["x"].rearrange("b (t p) d -> p (b t) d", p=P)).then_inc(s_acc, 16)
                with eng.Fori(0, B) as b:
                    for tt in range(TB):
                        t = TB * b + tt
                        hold(eng, s_sum, added(b, "rest", tt))
                        eng.dma_start(out.rearrange("b s d -> (b s) d")[bass.ds(t * P, P), :],
                                      acc[:, bass.ds(t, 1), :].rearrange("p a d -> p (a d)")).then_inc(s_out, 16)
                eng.wait_ge(s_out, 16 * NT)

            @block.gpsimd
            def _(eng):
                def low(step, r, turn):
                    hold(eng, s_wh, 4 * step + 4)
                    eng.tensor_tensor(w1l[:, bass.ds(step * G1, G1)], st1[r], w1h[:, bass.ds(step * G1, G1)],
                                      ALU.subtract).then_inc(s_wl, 1)
                    raw, w_hi, w_lo = second_weights(step, r)
                    eng.tensor_tensor(w_lo, raw, w_hi, ALU.subtract).then_inc(s_wl, 1)

                weight_steps(eng, low, 0, NW)
                for c in range(KD * B // 2):
                    k, g = c // B, c % B
                    eng.wait_ge(s_xth, c + 1)
                    eng.tensor_tensor(xT_lo[:, k, g * S:(g + 1) * S], xT32[:, k, g * S:(g + 1) * S],
                                      xT_hi[:, k, g * S:(g + 1) * S], ALU.subtract).then_inc(s_xtl, 1)
                eng.wait_ge(s_lists, 2)
                eng.wait_ge(s_xsd, 16)
                eng.wait_ge(s_xtl, KD * B)
                with eng.Fori(0, NBLK // UN) as i:
                    for r in range(UN):
                        hold(eng, s_T, UN * i + r + 1)
                        if r % RING == 0:
                            eng.tensor_copy(xg_idx[:, r:r + RING], token_of[:, bass.ds(UN * i + r, RING)]).then_inc(s_gi, 1)
                            hold(eng, s_gi, (UN // RING) * i + r // RING + 1)
                        eng.indirect_dma_start(
                            out=xg[:, r % RING, :], out_offset=None, in_=xs_dram,
                            in_offset=bass.IndirectOffsetOnAxis(ap=xg_idx[:, r:r + 1], axis=0)).then_inc(s_g[r % RING], 16)
                for r in range(RING):
                    eng.wait_ge(s_yd[r], 16 * (NBLK // RING))
                eng.wait_ge(s_L, NBLK)
                with eng.Fori(0, NT // ROWS) as i:
                    for r in range(ROWS):
                        hold(eng, s_sum, rows_added(i - 1, r))
                        eng.tensor_copy(row_idx[:, r, :].unsqueeze(2), row_of[:, :, bass.ds(ROWS * i + r, 1)]).then_inc(s_ri, 1)
                        hold(eng, s_ri, ROWS * i + r + 1)
                        for k in range(TOPK):
                            eng.indirect_dma_start(
                                out=rows[r][k], out_offset=None, in_=y_dram,
                                in_offset=bass.IndirectOffsetOnAxis(ap=row_idx[:, r, k:k + 1], axis=0)).then_inc(s_r[r], 16)

            @block.scalar
            def _(eng):
                eng.wait_ge(s_const, 16 * N_CONST)
                eng.activation(b1s[:, :], b1[:, :], ACT.Copy, scale=SC).then_inc(s_bias, 1)
                eng.activation(b1shs[:, :], b1sh[:, :], ACT.Copy, scale=SC / NS).then_inc(s_bias, 1)
                eng.wait_ge(s_d, 1)
                def high(step, r, n):
                    hold(eng, s_w[r], 32 * (n + 1))
                    for raw, w_hi in ((st1[r], w1h[:, bass.ds(step * G1, G1)]), second_weights(step, r)[0:2]):
                        eng.activation(w_hi, raw, ACT.Copy, scale=SC).then_inc(s_wh, 1)
                        eng.activation(raw, raw, ACT.Copy, scale=SC).then_inc(s_wh, 1)

                for c in range(2 * KD + NPROD):
                    w, k = (aw[c // KD], c % KD) if c < 2 * KD else (bw, c - 2 * KD)
                    eng.wait_ge(s_ab, c + 1)
                    eng.activation(w[0][:, k, :], ps[c][:, 0:D], ACT.Copy, scale=SC).then_inc(s_abs, 1)
                eng.wait_ge(s_d, 1)
                eng.activation(std[:, :], t16a[:, :], ACT.Sqrt).then_inc(s_std, 1)
                high(0, 0, 0)
                high(1, 1, 0)
                eng.wait_ge(s_abl, 2 * KD + NPROD)
                for c in range(KD * B):
                    k, g = c // B, c % B
                    eng.wait_ge(s_tr, c + 1)
                    eng.activation(xT32[:, k, g * S:(g + 1) * S], ps[c % 4][:, :], ACT.Copy).then_inc(s_xt, 1)
                for step in range(2, 5):
                    high(step, step % NST, step // NST)
                eng.wait_ge(s_dl, 1)
                eng.wait_ge(s_xt, KD * B)
                eng.activation(prb, dlog, ACT.Exp).then_inc(s_exp, 1)
                eng.wait_ge(s_xsd, 16)
                for c in range(KD * B):
                    k, g = c // B, c % B
                    eng.activation(xT_hi[:, k, g * S:(g + 1) * S], xT32[:, k, g * S:(g + 1) * S], ACT.Copy).then_inc(s_xth, 1)

                high(5, 2, 1)
                weight_steps(eng, high, 6, NW)

                eng.wait_ge(s_wl, 2 * (NW // NST * NST))
                eng.activation(ones_s, ones16[:, 0:1].to_broadcast([P, S]), ACT.Copy).then_inc(s_gtc, 1)
                eng.activation(gT[0][E:E + NS, :], ones16[E:E + NS, 0:1].to_broadcast([NS, TOK]), ACT.Copy,
                               scale=SC / NS).then_inc(s_gtc, 1)
                eng.activation(b2p[0][:, :], b2[:, :], ACT.Copy, scale=SC).then_inc(s_gtc, 1)
                for g in range(B):
                    eng.wait_ge(s_gt, g + 1)
                    eng.activation(gT[0][0:E, g * S:(g + 1) * S], ps[g][0:E, :], ACT.Copy, scale=SC).then_inc(s_gtc, 1)

                eng.wait_ge(s_bias, 2)
                eng.wait_ge(s_lists, 2)
                eng.wait_ge(s_xtl, KD * B)

                expert, load = experts_of(eng)

                def relu(i, r):
                    blk = UN * i + r
                    e = expert[r]
                    hold(eng, s_H, blk + 1)
                    for m in range(2):
                        eng.activation(h32[:, r % RING, m, :], ps_h[r % RING][:, m * P:(m + 1) * P], ACT.Relu,
                                       bias=b1s[:, bass.ds(2 * e + m, 1)], scale=1.0 / SC).then_inc(s_R, 1)

                def rows_out(i, r):
                    blk, slot, n = UN * i + r, r % RING, (UN // RING) * i + r // RING
                    after(eng, s_L, blk + 1)
                    after(eng, s_yd[slot], 16 * n)
                    eng.activation(yb[:, slot, :], ps_y[r % 2], ACT.Copy, scale=1.0 / (SC * SC)).then_inc(s_Y, 1)

                pipeline(eng, [(-3, rows_out), (0, relu)], load)

                eng.wait_ge(s_L, NBLK)
                eng.wait_ge(s_S, NBLK + S0)
                for r in range(RING):
                    eng.wait_ge(s_yd[r], 16 * (NBLK // RING))

                def spectra_out(b, first=False):
                    if not first:
                        hold(eng, s_v, STEPS * (b - 1) + 5)
                    for c in range(4):
                        dst = (q32, k32)[c // 2][:, c % 2, :]
                        hold(eng, s_sp, 4 * b + c + 1)
                        eng.activation(dst, ps[c][:, :], ACT.Copy, scale=1.0 / (SC * SC)).then_inc(s_spc, 1)
                        hold(eng, s_spc, 4 * b + c + 1)
                        eng.activation(work[c], dst, ACT.Square).then_inc(s_sq, 1)

                def roots(b):
                    hold(eng, s_nm, b + 1)
                    eng.activation(sv[:, :], ps[0][:, 0:NV], ACT.Sqrt).then_inc(s_rt, 1)

                def units(b, chunks):
                    hold(eng, s_shl, SH * b + 1)
                    for c in chunks:
                        n = SHC[c]
                        hold(eng, s_sh, SH * b + c + 1)
                        eng.activation(h32s[0:n, c, :], ps[6 + c % 2][0:n, :], ACT.Relu,
                                       bias=b1shs[0:n, c:c + 1], scale=1.0 / (SC * NS)).then_inc(s_shr, 1)

                def units_high(b):
                    for c, n in enumerate(SHC):
                        hold(eng, s_shr, SH * b + c + 1)
                        eng.activation(hs_hi[0:n, c, bass.ds(b * S, S)], h32s[0:n, c, :], ACT.Copy).then_inc(s_shh, 1)

                def inverse_norms(b):
                    hold(eng, s_rv, b + 1)
                    for n in (1, 0):
                        eng.activation(rvx[:, n, :].rearrange("p (h f) -> p h f", f=NF),
                                       rvi[:, n * TB * HEADS:(n + 1) * TB * HEADS].unsqueeze(2).to_broadcast([P, TB * HEADS, NF]),
                                       ACT.Copy).then_inc(s_rx, 1)

                def products_high(b):
                    for c in range(NPROD):
                        hold(eng, s_p32, NPROD * b + c + 1)
                        eng.activation(p_hi[:, c, bass.ds(b * S, S)], prod32[:, c, :], ACT.Copy).then_inc(s_ph, 1)

                spectra_out(0, first=True)
                roots(0)
                units(0, (0, 1))
                inverse_norms(0)
                units(0, (2,))
                units_high(0)
                with eng.Fori(0, B - 1) as b:
                    spectra_out(b + 1)
                    products_high(b)
                    roots(b + 1)
                    units(b + 1, (0, 1))
                    inverse_norms(b + 1)
                    units(b + 1, (2,))
                    units_high(b + 1)
                products_high(B - 1)

            @block.vector
            def _(eng):
                n_d = [0]

                def own(ins):
                    ins.then_inc(s_d, 1)
                    n_d[0] += 1
                    eng.wait_ge(s_d, n_d[0])

                for t in range(NT):
                    eng.wait_ge(s_x[t // TB], 16)
                    last = eng.bn_stats(stats[:, t, :], xn[:, t, :])
                    last.then_inc(s_ln, 1)
                for t in range(NT):
                    eng.wait_ge(s_ln, t + 1)
                    eng.bn_aggr(mv[:, t, :], stats[:, t, :]).then_inc(s_ln, 1)
                eng.wait_ge(s_ln, 2 * NT)
                var = mv[:, :, 1]
                own(eng.tensor_scalar(t16a[:, :], var, EPS, None, ALU.add))
                eng.wait_ge(s_std, 1)
                own(eng.reciprocal(t16b[:, :], std[:, :]))
                own(eng.tensor_tensor(t16b[:, :], t16b[:, :], t16a[:, :], ALU.mult))
                own(eng.tensor_tensor(t16b[:, :], t16b[:, :], std[:, :], ALU.add))
                own(eng.reciprocal(rstd[:, :], t16b[:, :]))
                own(eng.tensor_scalar(rstd[:, :], rstd[:, :], 2.0 * SC, None, ALU.mult))
                n_ln = 2 * NT
                for t in range(NT):
                    eng.tensor_scalar(xn[:, t, :], xn[:, t, :], mv[:, t, 0:1], rstd[:, t:t + 1],
                                      ALU.subtract, ALU.mult).then_inc(s_ln, 1)
                for c in range(2 * KD + NPROD):
                    w, k = (aw[c // KD], c % KD) if c < 2 * KD else (bw, c - 2 * KD)
                    eng.wait_ge(s_abs, c + 1)
                    eng.scalar_tensor_tensor(w[1][:, k, :], ps[c][:, 0:D], SC, w[0][:, k, :],
                                             ALU.mult, ALU.subtract).then_inc(s_abl, 1)
                for g in range(B):
                    t = slice(g * TB, (g + 1) * TB)
                    eng.wait_ge(s_ln, n_ln + (g + 1) * TB)
                    own(eng.tensor_copy(xs[:, t, 0, :], xn[:, t, :]))
                    eng.tensor_tensor(xs[:, t, 1, :], xn[:, t, :], xs[:, t, 0, :], ALU.subtract).then_inc(s_xs, TB)

                eng.wait_ge(s_log, 1)
                eng.wait_ge(s_tr, KD * B)
                own(eng.scalar_tensor_tensor(dlog, ps[4][:, :].rearrange("p (t e) -> p t e", t=NT), 1.0 / SC,
                                             rb[:, :].unsqueeze(1).to_broadcast([P, NT, E]), ALU.mult, ALU.add))
                own(eng.tensor_reduce(t16a[:, :], dlog, AX, ALU.max))
                eng.tensor_tensor(dlog, dlog, t16a[:, :].unsqueeze(2).to_broadcast([P, NT, E]),
                                  ALU.subtract).then_inc(s_dl, 1)
                eng.wait_ge(s_exp, 1)
                for t in range(NT):
                    own(eng.max(m8[:, t, :], prb[:, t, :]))
                    eng.max_index(i8[:, t, :], m8[:, t, :], prb[:, t, :]).then_inc(s_ln, 1)
                eng.wait_ge(s_ln, 4 * NT)
                own(eng.tensor_copy(i8f[:, :, :], i8[:, :, :]))
                for k in range(TOPK):
                    eng.tensor_tensor(OH[:, k, :, :], cf[:, C_IOTA_E:C_IOTA_E + E].unsqueeze(1).to_broadcast([P, NT, E]),
                                      i8f[:, :, k:k + 1].to_broadcast([P, NT, E]), ALU.is_equal).then_inc(s_mask, 1)
                own(eng.memset(ones_e[:, :], 1.0))
                own(eng.tensor_reduce(t16a[:, :], m8[:, :, 0:TOPK], AX, ALU.add))
                own(eng.reciprocal(t16b[:, :], t16a[:, :]))
                own(eng.tensor_tensor(gate[:, :, :], m8[:, :, 0:TOPK], t16b[:, :].unsqueeze(2).to_broadcast([P, NT, TOPK]), ALU.mult))
                eng.wait_ge(s_mask, TOPK)
                with nc.allow_low_precision(reason="sums of zeros and at most one 1"):
                    own(eng.tensor_reduce(mask, OH.rearrange("p k t e -> p t e k"), AX, ALU.add))
                own(eng.tensor_tensor(gates[:, :, :], prb, mask, ALU.mult))
                own(eng.tensor_tensor(gates[:, :, :], gates[:, :, :], t16b[:, :].unsqueeze(2).to_broadcast([P, NT, E]), ALU.mult))
                eng.sem_inc(s_gates, 1)
                eng.wait_ge(s_cnt, 1)
                totals = ps[6][:, :].rearrange("p (t e) -> p t e", t=NT)
                own(eng.memset(tmp[:, 0, :], 0.0))
                for t in range(NT):
                    dst = tmp[:, t + 1, :] if t < NT - 1 else cnt[:, :]
                    own(eng.tensor_tensor(dst, totals[:, t, :], tmp[:, t, :], ALU.add))
                own(eng.tensor_tensor(pos.rearrange("p t e -> p (t e)").rearrange("p (e t) -> p e t", e=E),
                                      cnt[:, :].unsqueeze(2).to_broadcast([P, E, NT]),
                                      cf[:, C_EDGE:C_EDGE + NT].unsqueeze(1).to_broadcast([P, E, NT]), ALU.is_gt))
                own(eng.tensor_reduce(nblk[:, :], pos.rearrange("p t e -> p (t e)").rearrange("p (e t) -> p e t", e=E), AX, ALU.add))
                own(eng.tensor_tensor_scan(cum[:, :], ones_e[:, :], nblk[:, :], 0.0, ALU.mult, ALU.add))
                own(eng.tensor_tensor(first[:, :], cum[:, :], nblk[:, :], ALU.subtract))
                own(eng.scalar_tensor_tensor(pos, first[:, :].unsqueeze(1).to_broadcast([P, NT, E]), float(P), tmp,
                                             ALU.mult, ALU.add))
                own(eng.tensor_tensor(pos, pos, ps[5][:, :].rearrange("p (t e) -> p t e", t=NT), ALU.add))
                start = n_d[0]
                for n in range(TOPK + 1):
                    if n < TOPK:
                        eng.wait_ge(s_d, start + max(0, 2 * n - 1))
                        eng.tensor_tensor((dlog, tmp)[n % 2], OH[:, n, :, :], pos, ALU.mult).then_inc(s_d, 1)
                    if n:
                        eng.wait_ge(s_d, start + max(1, 2 * n - 2))
                        eng.tensor_reduce(posk[:, n - 1, :], (dlog, tmp)[(n - 1) % 2], AX, ALU.add).then_inc(s_d, 1)
                n_d[0] += 2 * TOPK
                eng.wait_ge(s_d, n_d[0])
                own(eng.tensor_copy(row_of[:, :, :], posk[:, :, :]))
                own(eng.tensor_scalar(slot_i[:, 0, :, :], row_of[:, :, :], P - 1, None, ALU.bitwise_and))
                own(eng.tensor_scalar(slot_i[:, 1, :, :], row_of[:, :, :], 7, None, ALU.logical_shift_right))
                own(eng.tensor_copy(slot_f.rearrange("p h t k -> p h k t"), slot_i[:, :, :, :]))
                for t in range(NT):
                    if t >= 2:
                        eng.wait_ge(s_tab, TOPK * (t - 1))
                    n_d[0] += 1
                    for part, dst, sem_ in ((1, oh_blk, s_d), (0, oh_slot, s_oh)):
                        eng.tensor_tensor(dst[:, t % 2, :, :], counting,
                                          slot_f[:, part, t, :].unsqueeze(1).to_broadcast([P, P, TOPK]),
                                          ALU.is_equal).then_inc(sem_, 1)
                    eng.wait_ge(s_d, n_d[0])
                    eng.tensor_scalar(oh_blk[:, t % 2, :, :], oh_blk[:, t % 2, :, :], cf[:, C_TOKID + t:C_TOKID + t + 1], None,
                                      ALU.mult).then_inc(s_oh, 1)
                own(eng.tensor_scalar(nblk[:, :], cum[:, :], cf[:, C_PIDX:C_PIDX + 1], None, ALU.is_le))
                own(eng.tensor_reduce(first[:, 0:1], nblk[:, :], AX, ALU.add))
                eng.tensor_scalar(ebc[:, :], first[:, 0:1], float(E - 1), None, ALU.min).then_inc(s_eb, 1)
                eng.wait_ge(s_tab, NT * TOPK)
                eng.tensor_copy(token_of[:, :], ps[7][:, 0:NBLK]).then_inc(s_lists, 1)
                eng.wait_ge(s_ebr, 1)
                own(eng.tensor_copy(parts_of[:, :, :], ps[6][0:1, 0:2 * NWORD].rearrange("p (h w) -> p h w", h=2)))
                own(eng.tensor_scalar(parts_of[:, 1, :], parts_of[:, 1, :], EBITS * LOW, None, ALU.logical_shift_left))
                eng.tensor_tensor(experts[:, :], parts_of[:, 0, :], parts_of[:, 1, :], ALU.bitwise_or).then_inc(s_lists, 1)

                for c in range(KD * B // 2, KD * B):
                    k, g = c // B, c % B
                    eng.wait_ge(s_xth, c + 1)
                    eng.tensor_tensor(xT_lo[:, k, g * S:(g + 1) * S], xT32[:, k, g * S:(g + 1) * S],
                                      xT_hi[:, k, g * S:(g + 1) * S], ALU.subtract).then_inc(s_xtl, 1)
                eng.wait_ge(s_wl, 2 * NW)
                eng.wait_ge(s_gtc, 3)
                eng.scalar_tensor_tensor(b2p[1][:, :], b2[:, :], SC, b2p[0][:, :], ALU.mult, ALU.subtract).then_inc(s_gtl, 1)
                for g in range(B):
                    eng.wait_ge(s_gtc, g + 4)
                    eng.scalar_tensor_tensor(gT[1][0:E, g * S:(g + 1) * S], ps[g][0:E, :], SC, gT[0][0:E, g * S:(g + 1) * S],
                                             ALU.mult, ALU.subtract).then_inc(s_gtl, 1)

                def tokens_out(i, r):
                    blk = UN * i + r
                    eng.wait_ge(s_T, blk + RING + 1)
                    eng.tensor_copy(xgT[:, r % RING, :, :].rearrange("p c s -> p (c s)"), ps_x[r % 2]).then_inc(s_X, 1)

                def units_hi(i, r):
                    blk = UN * i + r
                    eng.wait_ge(s_R, 2 * blk + 2)
                    eng.tensor_copy(h_hi[:, r % RING, :, :], h32[:, r % RING, :, :]).then_inc(s_C, 1)

                def units_lo(i, r):
                    blk = UN * i + r
                    eng.wait_ge(s_C, blk + 1)
                    eng.tensor_tensor(h_lo[:, r % RING, :, :], h32[:, r % RING, :, :], h_hi[:, r % RING, :, :],
                                      ALU.subtract).then_inc(s_S, 1)

                eng.wait_ge(s_xtl, KD * B)
                pipeline(eng, [(-1, units_hi), (2, tokens_out), (-1, units_lo)])


                def attention(b):
                    def needs(n):
                        hold(eng, s_v, STEPS * b + n)

                    def inverse_norms(step):
                        if step == 0:
                            hold(eng, s_rt, b + 1)
                            eng.reciprocal(rv[:, :], sv[:, :]).then_inc(s_v, 1)
                            return
                        needs(step)
                        if step == 1:
                            eng.tensor_tensor(rv[:, :], rv[:, :], ps[0][:, 0:NV], ALU.mult).then_inc(s_v, 1)
                        elif step == 2:
                            eng.tensor_tensor(rv[:, :], rv[:, :], sv[:, :], ALU.add).then_inc(s_v, 1)
                        else:
                            eng.reciprocal(rvi[:, :], rv[:, :]).then_inc(s_rv, 1)

                    def normalise(step):
                        hold(eng, s_ex, 2 * b + step + 1)
                        if step == 0:
                            ins = eng.tensor_tensor(kn32, k32, ps[1][:, :].unsqueeze(1).to_broadcast([P, 2, S]), ALU.mult)
                        else:
                            ins = eng.scalar_tensor_tensor(qn32, q32, SC, ps[2][:, :].unsqueeze(1).to_broadcast([P, 2, S]),
                                                           ALU.mult, ALU.mult)
                        ins.then_inc(s_v, 1)

                    def sum_over_time(c):
                        needs(4)
                        eng.tensor_tensor_scan(kc32[:, c, :], ones_s, kn32[:, c, :], 0.0, ALU.mult, ALU.add).then_inc(s_v, 1)

                    def products(step):
                        needs(9 if step == 4 else 7)
                        if step < 2:
                            eng.tensor_tensor(work[4 + step], qn32[:, step, :], kc32[:, 1 - step, :], ALU.mult).then_inc(s_v, 1)
                        elif step < 4:
                            c = step - 2
                            eng.tensor_tensor(prod32[:, c, :], qn32[:, c, :], kc32[:, c, :], ALU.mult).then_inc(s_p32, 1)
                        else:
                            eng.tensor_tensor(prod32[:, 2, :], work[4], work[5], ALU.add).then_inc(s_p32, 1)

                    def units_low(c):
                        n = SHC[c]
                        hold(eng, s_shh, SH * b + c + 1)
                        eng.tensor_tensor(hs_lo[0:n, c, bass.ds(b * S, S)], h32s[0:n, c, :], hs_hi[0:n, c, bass.ds(b * S, S)],
                                          ALU.subtract).then_inc(s_shl, 1)

                    def products_low(c):
                        hold(eng, s_ph, NPROD * b + c + 1)
                        eng.tensor_tensor(p_lo[:, c, bass.ds(b * S, S)], prod32[:, c, :], p_hi[:, c, bass.ds(b * S, S)],
                                          ALU.subtract).then_inc(s_pl, 1)

                    return ([(inverse_norms, n) for n in range(4)] +
                            [(normalise, 0), (normalise, 1), (sum_over_time, 0), (sum_over_time, 1)] +
                            [(products, n) for n in range(5)] + [(units_low, c) for c in range(SH)] +
                            [(products_low, c) for c in range(NPROD)])

                def additions(b, which, steps):
                    steps = [(lo, hi, list(some)) for lo, hi, some in steps]
                    for n, at in enumerate(which):
                        kind, tt, *k = ADDITIONS[at]
                        t = TB * b + tt + (LATE if kind == "rows" else 0)
                        tile = acc[:, bass.ds(t, 1), :].rearrange("p a d -> p (a d)")
                        if kind == "rows":
                            slot = (tt + LATE) % ROWS
                            if k[0] == 0:
                                hold(eng, s_r[slot], 16 * TOPK * (b + (tt + LATE) // ROWS + 1))
                            else:
                                hold(eng, s_sum, added(b, *ADDITIONS[at]) - 1)
                            g = gate[:, bass.ds(t, 1), k[0]:k[0] + 1].rearrange("p a k -> p (a k)")
                            ins = eng.scalar_tensor_tensor(tile, rows[slot][k[0]], g, tile, ALU.mult, ALU.add)
                        else:
                            hold(eng, s_o, t + 1)
                            ins = eng.scalar_tensor_tensor(tile, ps[4 + tt % 2][:, 0:D], 1.0 / (SC * SC), tile,
                                                           ALU.mult, ALU.add)
                        ins.then_inc(s_sum, (which[n + 1] if n + 1 < len(which) else TURN) - at)
                        for lo, hi, some in steps:
                            if lo <= n < hi:
                                for _ in range(-(-len(some) // (hi - n))):
                                    f, arg = some.pop(0)
                                    f(arg)
                    assert not any(some for lo, hi, some in steps)

                every = range(TURN)
                eng.wait_ge(s_L, NBLK)
                eng.wait_ge(s_gtl, 1 + B)
                eng.wait_ge(s_acc, 16)
                early = attention(0)
                additions(-1, [n for n in every if ADDITIONS[n][0] == "rows" and ADDITIONS[n][1] >= TB - LATE],
                          [(TOPK, LATE * TOPK, early[:TOPK])])
                additions(0, every, [(0, TOPK, early[TOPK:]), (START, TURN, attention(1))])
                with eng.Fori(1, B - 1) as b:
                    additions(b, every, [(START, TURN, attention(b + 1))])
                additions(B - 1, [n for n in every if ADDITIONS[n][0] == "rest" or ADDITIONS[n][1] < TB - LATE], [])

            @block.tensor
            def _(eng):
                eng.sem_inc(s_S, S0)
                eng.sem_inc(s_Y, Y0)
                eng.sem_inc(s_T, RING)
                eng.sem_inc(s_sum, CREDIT)
                eng.sem_inc(s_shl, 1)

                eng.wait_ge(s_raw, 16 * N_RAW)
                for c in range(2 * KD + NPROD):
                    for k in range(KD):
                        if c < 2 * KD:
                            m = c % KD
                            ins = eng.matmul(ps[c][:, 0:D], w_raw[c // KD][:, k, m * P:(m + 1) * P], f_mat[:, k, :],
                                             start=(k == 0), stop=(k == KD - 1))
                        else:
                            m = c - 2 * KD
                            ins = eng.matmul(ps[c][:, 0:D], g_mat[:, k, m * P:(m + 1) * P], w_raw[2][:, k, :],
                                             start=(k == 0), stop=(k == KD - 1))
                    ins.then_inc(s_ab, 1)

                eng.wait_ge(s_const, 16 * N_CONST)
                eng.wait_ge(s_abl, 2 * KD + NPROD)
                for c in range(KD * B):
                    k, g = c // B, c % B
                    eng.wait_ge(s_ln, 2 * NT + (g + 1) * TB)
                    if c >= 4:
                        eng.wait_ge(s_xt, c - 3)
                    for tt in range(TB):
                        ins = eng.transpose(ps[c % 4][:, tt * P:(tt + 1) * P], xn[:, g * TB + tt, k * P:(k + 1) * P], ident32)
                    ins.then_inc(s_tr, 1)
                eng.wait_ge(s_xt, KD * B)
                for t in range(NT):
                    for k in range(KD):
                        ins = eng.matmul(ps[4][:, t * E:(t + 1) * E], xT32[:, k, t * P:(t + 1) * P], rw[:, k, :],
                                         start=(k == 0), stop=(k == KD - 1))
                ins.then_inc(s_log, 1)
                for k in range(TOPK):
                    eng.wait_ge(s_mask, k + 1)
                    flat = OH[:, k, :, :].rearrange("p t e -> p (t e)")
                    eng.matmul(ps[5][:, :], tri, flat, start=(k == 0), stop=(k == TOPK - 1))
                    ins = eng.matmul(ps[6][:, :], ones16, flat, start=(k == 0), stop=(k == TOPK - 1))
                ins.then_inc(s_cnt, 1)
                for t in range(NT):
                    eng.wait_ge(s_oh, 2 * t + 2)
                    for k in range(TOPK):
                        eng.matmul(ps[7][:, 0:P], oh_slot[:, t % 2, :, k], oh_blk[:, t % 2, :, k],
                                   start=(t == 0 and k == 0), stop=(t == NT - 1 and k == TOPK - 1)).then_inc(s_tab, 1)
                eng.wait_ge(s_eb, 1)
                eng.matmul(ps[6][0:1, 0:2 * NWORD], ebc[:, :], cf[:, C_PACK:C_ALL], start=True, stop=True).then_inc(s_ebr, 1)

                def transposes(i, r):
                    eng.wait_ge(s_g[r % RING], 16 * ((UN // RING) * i + r // RING + 1))
                    for c in range(4):
                        ins = eng.transpose(ps_x[r % 2][:, c * P:(c + 1) * P], xg[:, r % RING, c * P:(c + 1) * P], ident16)
                    ins.then_inc(s_T, 1)

                expert, load = experts_of(eng)

                def layer1(i, r):
                    blk = UN * i + r
                    e = expert[r]
                    eng.wait_ge(s_X, blk + 1)
                    for m in range(2):
                        j = 0
                        for k in range(KD):
                            for w, x_part in ((w1h, k), (w1h, KD + k), (w1l, k)):
                                ins = eng.matmul(ps_h[r % RING][:, m * P:(m + 1) * P],
                                                 w[:, k * HID + m * HC:][:, bass.ds(e * (KD * HID), HC)],
                                                 xgT[:, r % RING, x_part, :], start=(j == 0), stop=(j == 3 * KD - 1))
                                j += 1
                                if m == 0 and j == 1 and not (isinstance(i, int) and blk < Y0):
                                    eng.wait_ge(s_Y, blk + 1)
                    ins.then_inc(s_H, 1)

                def layer2(i, r):
                    blk = UN * i + r
                    e = expert[r]
                    if isinstance(i, int) and blk >= NBLK - S0:
                        eng.wait_ge(s_Y, blk + S0 + 1)
                    eng.wait_ge(s_S, blk + S0 + 1)
                    j = 0
                    for m in range(2):
                        for h, w in ((h_hi, w2h), (h_hi, w2l), (h_lo, w2h)):
                            ins = eng.matmul(ps_y[r % 2], h[:, r % RING, m, :], w[:, m * D:][:, bass.ds(e * (2 * D), D)],
                                             start=(j == 0), stop=(j == 5))
                            j += 1
                    ins.then_inc(s_L, 1)

                eng.wait_ge(s_wl, 2 * NW)
                eng.wait_ge(s_gates, 1)
                for g in range(B):
                    for tt in range(TB):
                        ins = eng.transpose(ps[g][0:E, tt * P:(tt + 1) * P], gates[:, g * TB + tt, :], ident32)
                    ins.then_inc(s_gt, 1)
                eng.wait_ge(s_gtl, 1 + B)
                eng.wait_ge(s_lists, 2)
                pipeline(eng, [(0, layer1), (-3, layer2), (2, transposes)], load)

                eng.wait_ge(s_R, 2 * NBLK)
                eng.wait_ge(s_Y, NBLK + Y0)

                def spectra(b, first=False):
                    if not first:
                        eng.wait_ge(s_rv, b)
                        eng.wait_ge(s_v, STEPS * (b - 1) + 5)
                    for c in range(4):
                        if not first:
                            eng.wait_ge(s_spc, 4 * b - 4 + c + 1)
                        j = 0
                        w, m = aw[c // 2], c % 2
                        for k in range(KD):
                            for wp, xp in ((w[0], xT_hi), (w[0], xT_lo), (w[1], xT_hi)):
                                ins = eng.matmul(ps[c][:, :], wp[:, k, m * P:(m + 1) * P], xp[:, k, bass.ds(b * S, S)],
                                                 start=(j == 0), stop=(j == 3 * KD - 1))
                                j += 1
                        ins.then_inc(s_sp, 1)

                def shared_units(b, chunks, first=False):
                    for c in chunks:
                        if not (first and c < 2):
                            eng.wait_ge(s_shr, SH * b + max(0, c - 1))
                        j = 0
                        units = slice(c * P, c * P + SHC[c])
                        for k in range(KD):
                            for wp, xp in ((w1sh, xT_hi), (w1sh, xT_lo), (w1sl, xT_hi)):
                                ins = eng.matmul(ps[6 + c % 2][0:SHC[c], :], wp[:, k, units], xp[:, k, bass.ds(b * S, S)],
                                                 start=(j == 0), stop=(j == 3 * KD - 1))
                                j += 1
                        ins.then_inc(s_sh, 1)

                def norms(b):
                    eng.wait_ge(s_sq, 4 * b + 4)
                    for n in range(2):
                        for tt in range(TB):
                            at = (n * TB + tt) * HEADS
                            for c in range(2):
                                ins = eng.matmul(ps[0][:, at:at + HEADS], work[2 * n + c][:, tt * P:(tt + 1) * P], headsum,
                                                 start=(c == 0), stop=(c == 1))
                    ins.then_inc(s_nm, 1)

                def spread(b):
                    for j, n in enumerate((1, 0)):
                        eng.wait_ge(s_rx, 2 * b + j + 1)
                        for tt in range(TB):
                            ins = eng.transpose(ps[1 + j][:, tt * P:(tt + 1) * P], rvx[:, n, tt * P:(tt + 1) * P], ident32)
                        ins.then_inc(s_ex, 1)

                def second_layers(b, tiles):
                    eng.wait_ge(s_pl, NPROD * b + NPROD)
                    eng.wait_ge(s_shl, SH * b + SH + 1)
                    for tt in tiles:
                        t = TB * b + tt
                        eng.wait_ge(s_sum, added(b, "rest", tt - 2) if tt >= 2 else added(b - 1, "rest", TB + tt - 2))
                        tok = bass.ds(t * P, P)
                        parts = [(p_[:, c, tok], w[:, c, :]) for c in range(NPROD) for p_, w in ((p_hi, bw[0]), (p_hi, bw[1]), (p_lo, bw[0]))]
                        for c, n in enumerate(SHC):
                            parts += [(h_[0:n, c, tok], w[0:n, c * D:(c + 1) * D])
                                      for h_, w in ((hs_hi, w2sh), (hs_hi, w2sl), (hs_lo, w2sh))]
                        parts += [(gT[0][:, tok], b2p[0][:, :]), (gT[0][:, tok], b2p[1][:, :]), (gT[1][0:E, tok], b2p[0][0:E, :])]
                        for j, (lhs, rhs) in enumerate(parts):
                            ins = eng.matmul(ps[4 + tt % 2][:, 0:D], lhs, rhs, start=(j == 0), stop=(j == len(parts) - 1))
                        ins.then_inc(s_o, 1)

                for b in range(2):
                    spectra(b, first=b == 0)
                    shared_units(b, (0, 1), first=b == 0)
                    norms(b)
                    if b == 0:
                        spread(b)
                        shared_units(b, (2,))

                def batch(b, last=False):
                    second_layers(b, (0, 1))
                    spread(b + 1)
                    shared_units(b + 1, (2,))
                    second_layers(b, (2,))
                    if not last:
                        spectra(b + 2)
                        shared_units(b + 2, (0, 1))
                    second_layers(b, (3,))
                    if not last:
                        norms(b + 2)

                with eng.Fori(0, B - 2) as b:
                    batch(b)
                batch(B - 2, last=True)
                second_layers(B - 1, range(TB))


def constants():
    cf = np.zeros((P, C_ALL), np.float32)
    p = np.arange(P)
    cf[:, C_IOTA_E:C_IOTA_E + E] = np.arange(E)
    cf[:, C_EDGE:C_EDGE + NT] = np.arange(NT) * P
    cf[:, C_PIDX] = p
    cf[:, C_TOKID:C_TOKID + NT] = np.arange(NT)[None, :] * P + p[:, None]
    cf[:, C_IDENT:C_IDENT + P] = np.eye(P)
    cf[:, C_HEADSUM:C_PACK] = (p[:, None] // NF) == np.arange(HEADS)[None, :]
    for w in range(NWORD):
        for j in range(WBLK):
            blk = UN * (w // 2) - BACK + WBLK * (w % 2) + j
            if blk >= 0:
                cf[blk, C_PACK + (j >= LOW) * NWORD + w] = 2 ** (EBITS * (j % LOW))
    ch = np.zeros((P, H_ALL), np.float16)
    ch[:, H_COUNT:] = np.repeat(p, TOPK)
    ch[:, H_TRI:H_TRI + P] = p[:, None] < p[None, :]
    ch[:, H_ONES:H_ONES + P] = 1
    ch[:, H_IDENT:H_IDENT + P] = np.eye(P)
    i, f = np.arange(HD)[:, None], np.arange(NF)[None, :]
    ang = 2 * np.pi * i * f / HD
    alt = (-1.0) ** np.arange(HD)
    re = np.sqrt(2.0 / HD) * np.cos(ang)
    im = -np.sqrt(2.0 / HD) * np.sin(ang)
    re[:, 0] = 1 / np.sqrt(HD)
    im[:, 0] = alt / np.sqrt(HD)
    rr, ii, ri = np.cos(ang) / HD, -np.cos(ang) / HD, -np.sin(ang) / HD
    ii[:, 0] = alt / HD
    ri[:, 0] = 0
    fm = np.zeros((HEADS, HD, 2, HEADS, NF))
    gm = np.zeros((HEADS, HD, NPROD, HEADS, NF))
    for h in range(HEADS):
        for c, m in enumerate((re, im)):
            fm[h, :, c, h, :] = m
        for c, m in enumerate((rr, ii, ri)):
            gm[h, :, c, h, :] = 4 * m
    chunk = lambda m: np.ascontiguousarray(m.reshape(KD, P, -1).transpose(1, 0, 2).astype(np.float32))
    return {"cf": cf, "ch": ch, "f_mat": chunk(fm), "g_mat": chunk(gm)}


def kernel(**inputs):
    import concourse.bacc as bacc
    from concourse.bass_utils import run_bass_kernel_spmd

    v = {n.replace("L0_", ""): np.asarray(t) for n, t in inputs.items()}
    lay = np.ascontiguousarray
    chunk = lambda m: lay(m.reshape(KD, P, -1).transpose(1, 0, 2))
    def first_layers(w):
        return w.reshape(-1, KD, P, w.shape[-1]).transpose(2, 0, 1, 3).reshape(P, -1)

    def units_by_chunk(m):
        m = np.concatenate([m, np.zeros((SH * P - NS * HID, m.shape[1]), m.dtype)])
        return lay(m.reshape(SH, P, -1).transpose(1, 0, 2).reshape(P, -1))

    arrays = {
        "x": lay(v["attn_x"]), "wq": chunk(v["attn_W_q"]), "wkv": chunk(v["attn_W_kv"]), "woT": chunk(v["attn_W_o"].T),
        "rw": chunk(v["ffn_router_w"]), "rb": lay(v["ffn_router_b"]),
        "w1": lay(np.concatenate([first_layers(v["ffn_rw1"]),
                                  first_layers(v["ffn_sw1"].transpose(1, 0, 2).reshape(1, D, -1))], axis=1)),
        "w2": lay(v["ffn_rw2"].reshape(E, 2, HC, D).transpose(2, 0, 1, 3).reshape(HC, -1)),
        "w2s": units_by_chunk(v["ffn_sw2"].reshape(-1, D)),
        "b1": lay(v["ffn_rb1"].reshape(E, 2, HC).transpose(2, 0, 1).reshape(HC, -1)),
        "b1s": units_by_chunk(v["ffn_sb1"].reshape(-1, 1)),
        "rb2": lay(v["ffn_rb2"]), "sb2": lay(v["ffn_sb2"]), **constants(),
    }
    nc = bacc.Bacc("TRN2", target_bir_lowering=False, num_devices=1)
    aps = {n: nc.dram_tensor("in_" + n, t.shape, mybir.dt.from_np(t.dtype), kind="ExternalInput").ap()
           for n, t in arrays.items()}
    out = nc.dram_tensor("out", (B, S, D), F32, kind="ExternalOutput").ap()
    build(nc, aps, out)
    r = run_bass_kernel_spmd(nc, [{"in_" + n: t for n, t in arrays.items()}], core_ids=[0])
    return r.results[0]["out"]
```
